# Optimizing a Trainium2 kernel written in Bass

```python
import numpy as np
import jax
import jax.numpy as jnp

def _softmax(x, axis=-1):
    return jax.nn.softmax(x, axis=axis)

def _gelu(x):
    return jax.nn.gelu(x, approximate=True)

def _silu(x):
    return jax.nn.silu(x)

def _sigmoid(x):
    return jax.nn.sigmoid(x)

def _layernorm(x, axis=-1, eps=1e-05):
    m = jnp.mean(x, axis=axis, keepdims=True)
    v = jnp.var(x, axis=axis, keepdims=True)
    return (x - m) / jnp.sqrt(v + eps)

def _scatter_add(tgt, idx, src, axis=0):
    return tgt.at[idx].add(src)

def _segment_sum(src, seg, n):
    return jax.ops.segment_sum(src, seg, n)
kernel_name = 'mk_gnn_ffn_d1_gnn_r8_0d0028'

def setup_inputs(seed: int=0):
    np.random.seed(seed)
    _w = jnp.asarray

    def _rec_inputs():
        import jax
        import jax.numpy as jnp
        _gk = jax.random.key(seed)
        x = -7.329e-05 + 0.9999 * jax.random.normal(jax.random.fold_in(_gk, 1), (1250, 512), jnp.float32)
        src = jax.random.randint(jax.random.fold_in(_gk, 2), (20000,), 0, 1250, jnp.int32)
        dst = jnp.minimum((1250 * jax.random.uniform(jax.random.fold_in(_gk, 3), (20000,)) ** 2.0).astype(jnp.int32), 9999)
        _o = jnp.argsort(dst, stable=True)
        src = src[_o]
        dst = dst[_o]
        return (x, src, dst)
    x, src, dst = _rec_inputs()

    def _L0_gnn_setup():
        import jax, jax.numpy as jnp
        import numpy as np
        N = 12500
        E = 100000
        D_IN = 512
        D_OUT = 512
        EPS = 1e-05
        key = jax.random.key(seed)
        k = jax.random.split(key, 7)
        x = jax.random.normal(k[0], (N, D_IN), dtype=jnp.float32)
        edge_index = jax.random.randint(k[1], (2, E), 0, N, dtype=jnp.int64)
        W_l = jax.random.normal(k[2], (D_OUT, D_IN), dtype=jnp.float32) * 0.02
        b_l = jnp.zeros((D_OUT,), dtype=jnp.float32)
        W_r = jax.random.normal(k[3], (D_OUT, D_IN), dtype=jnp.float32) * 0.02
        gamma = jnp.ones((D_OUT,), dtype=jnp.float32)
        beta = jnp.zeros((D_OUT,), dtype=jnp.float32)
        return {'x': x, 'edge_index': edge_index, 'W_l': W_l, 'b_l': b_l, 'W_r': W_r, 'gamma': gamma, 'beta': beta}
    _L0_gnn_all = _L0_gnn_setup()
    _L0_gnn_in = {k: v for k, v in _L0_gnn_all.items() if k in ('W_l', 'b_l', 'W_r', 'gamma', 'beta')}
    del _L0_gnn_all

    def _L0_ffn_setup():
        import jax, jax.numpy as jnp
        import numpy as np
        E = 512
        H = 8
        D = E // H
        HID = 256
        NE = 4
        TOPK = 2
        EPS = 1e-05
        NEG = -1000000000.0

        def _ln(x, w, b):
            mu = jnp.mean(x, axis=-1, keepdims=True)
            var = jnp.mean(jnp.square(x - mu), axis=-1, keepdims=True)
            return (x - mu) * jax.lax.rsqrt(var + EPS) * w + b

        def _expert(xf, mask, ln1_w, ln1_b, ipw, ipb, opw, opb, ln2_w, ln2_b, w1, b1, w2, b2):
            T = xf.shape[0]
            h = _ln(xf, ln1_w, ln1_b)
            qkv = h @ ipw.T + ipb
            q, k, v = jnp.split(qkv, 3, axis=-1)
            q = q.reshape(T, H, D).transpose(1, 0, 2)
            k = k.reshape(T, H, D).transpose(1, 0, 2)
            v = v.reshape(T, H, D).transpose(1, 0, 2)
            scores = jnp.einsum('htd,hsd->hts', q, k) / jnp.sqrt(jnp.asarray(D, xf.dtype))
            scores = jnp.where(mask[None, None, :], scores, NEG)
            a = jax.nn.softmax(scores, axis=-1)
            o = jnp.einsum('hts,hsd->htd', a, v).transpose(1, 0, 2).reshape(T, E)
            o = o @ opw.T + opb
            x1 = xf + o
            h2 = _ln(x1, ln2_w, ln2_b)
            m = jax.nn.gelu(h2 @ w1.T + b1, approximate=False) @ w2.T + b2
            return x1 + m
        key = jax.random.key(seed)
        ks = jax.random.split(key, 16)
        s = 0.02
        inp = {'x': jax.random.normal(ks[0], (4, 512, E), dtype=jnp.float32), 'gate_w': jax.random.normal(ks[1], (NE, E), dtype=jnp.float32) * s, 'gate_b': jnp.zeros((NE,), jnp.float32), 'ln1_w': jnp.ones((NE, E), jnp.float32), 'ln1_b': jnp.zeros((NE, E), jnp.float32), 'in_proj_w': jax.random.normal(ks[2], (NE, 3 * E, E), dtype=jnp.float32) * s, 'in_proj_b': jnp.zeros((NE, 3 * E), jnp.float32), 'out_proj_w': jax.random.normal(ks[3], (NE, E, E), dtype=jnp.float32) * s, 'out_proj_b': jnp.zeros((NE, E), jnp.float32), 'ln2_w': jnp.ones((NE, E), jnp.float32), 'ln2_b': jnp.zeros((NE, E), jnp.float32), 'mlp_w1': jax.random.normal(ks[4], (NE, HID, E), dtype=jnp.float32) * s, 'mlp_b1': jnp.zeros((NE, HID), jnp.float32), 'mlp_w2': jax.random.normal(ks[5], (NE, E, HID), dtype=jnp.float32) * s, 'mlp_b2': jnp.zeros((NE, E), jnp.float32)}
        return inp
    _L0_ffn_all = _L0_ffn_setup()
    _L0_ffn_in = {k: v for k, v in _L0_ffn_all.items() if k in ('gate_w', 'gate_b', 'ln1_w', 'ln1_b', 'in_proj_w', 'in_proj_b', 'out_proj_w', 'out_proj_b', 'ln2_w', 'ln2_b', 'mlp_w1', 'mlp_b1', 'mlp_w2', 'mlp_b2')}
    del _L0_ffn_all
    return {'x': x, 'src': src, 'dst': dst, 'L0_gnn_W_l': _L0_gnn_in['W_l'], 'L0_gnn_b_l': _L0_gnn_in['b_l'], 'L0_gnn_W_r': _L0_gnn_in['W_r'], 'L0_gnn_gamma': _L0_gnn_in['gamma'], 'L0_gnn_beta': _L0_gnn_in['beta'], 'L0_ffn_gate_w': _L0_ffn_in['gate_w'], 'L0_ffn_gate_b': _L0_ffn_in['gate_b'], 'L0_ffn_ln1_w': _L0_ffn_in['ln1_w'], 'L0_ffn_ln1_b': _L0_ffn_in['ln1_b'], 'L0_ffn_in_proj_w': _L0_ffn_in['in_proj_w'], 'L0_ffn_in_proj_b': _L0_ffn_in['in_proj_b'], 'L0_ffn_out_proj_w': _L0_ffn_in['out_proj_w'], 'L0_ffn_out_proj_b': _L0_ffn_in['out_proj_b'], 'L0_ffn_ln2_w': _L0_ffn_in['ln2_w'], 'L0_ffn_ln2_b': _L0_ffn_in['ln2_b'], 'L0_ffn_mlp_w1': _L0_ffn_in['mlp_w1'], 'L0_ffn_mlp_b1': _L0_ffn_in['mlp_b1'], 'L0_ffn_mlp_w2': _L0_ffn_in['mlp_w2'], 'L0_ffn_mlp_b2': _L0_ffn_in['mlp_b2']}

def reference(x, src, dst, L0_gnn_W_l, L0_gnn_b_l, L0_gnn_W_r, L0_gnn_gamma, L0_gnn_beta, L0_ffn_gate_w, L0_ffn_gate_b, L0_ffn_ln1_w, L0_ffn_ln1_b, L0_ffn_in_proj_w, L0_ffn_in_proj_b, L0_ffn_out_proj_w, L0_ffn_out_proj_b, L0_ffn_ln2_w, L0_ffn_ln2_b, L0_ffn_mlp_w1, L0_ffn_mlp_b1, L0_ffn_mlp_w2, L0_ffn_mlp_b2):
    import jax
    import jax.numpy as jnp

    def _L0_gnn_ref(x, edge_index, W_l, b_l, W_r, gamma, beta):
        import jax, jax.numpy as jnp
        import numpy as np
        N = 12500
        E = 100000
        D_IN = 512
        D_OUT = 512
        EPS = 1e-05
        n = x.shape[0]
        src, dst = (edge_index[0], edge_index[1])
        summed = jax.ops.segment_sum(x[src], dst, num_segments=n)
        cnt = jax.ops.segment_sum(jnp.ones((src.shape[0],), x.dtype), dst, num_segments=n)
        aggr = summed / jnp.maximum(cnt, 1.0)[:, None]
        h = aggr @ W_l.T + b_l + x @ W_r.T
        mu = jnp.mean(h, axis=0)
        var = jnp.mean(jnp.square(h - mu), axis=0)
        h_norm = (h - mu) * jax.lax.rsqrt(var + EPS) * gamma + beta
        return jax.nn.relu(h_norm)

    def _L0_ffn_ref(x, gate_w, gate_b, ln1_w, ln1_b, in_proj_w, in_proj_b, out_proj_w, out_proj_b, ln2_w, ln2_b, mlp_w1, mlp_b1, mlp_w2, mlp_b2):
        import jax, jax.numpy as jnp
        import numpy as np
        E = 512
        H = 8
        D = E // H
        HID = 256
        NE = 4
        TOPK = 2
        EPS = 1e-05
        NEG = -1000000000.0

        def _ln(x, w, b):
            mu = jnp.mean(x, axis=-1, keepdims=True)
            var = jnp.mean(jnp.square(x - mu), axis=-1, keepdims=True)
            return (x - mu) * jax.lax.rsqrt(var + EPS) * w + b

        def _expert(xf, mask, ln1_w, ln1_b, ipw, ipb, opw, opb, ln2_w, ln2_b, w1, b1, w2, b2):
            T = xf.shape[0]
            h = _ln(xf, ln1_w, ln1_b)
            qkv = h @ ipw.T + ipb
            q, k, v = jnp.split(qkv, 3, axis=-1)
            q = q.reshape(T, H, D).transpose(1, 0, 2)
            k = k.reshape(T, H, D).transpose(1, 0, 2)
            v = v.reshape(T, H, D).transpose(1, 0, 2)
            scores = jnp.einsum('htd,hsd->hts', q, k) / jnp.sqrt(jnp.asarray(D, xf.dtype))
            scores = jnp.where(mask[None, None, :], scores, NEG)
            a = jax.nn.softmax(scores, axis=-1)
            o = jnp.einsum('hts,hsd->htd', a, v).transpose(1, 0, 2).reshape(T, E)
            o = o @ opw.T + opb
            x1 = xf + o
            h2 = _ln(x1, ln2_w, ln2_b)
            m = jax.nn.gelu(h2 @ w1.T + b1, approximate=False) @ w2.T + b2
            return x1 + m
        B, N, _ = x.shape
        T = B * N
        xf = x.reshape(T, E)
        logits = xf @ gate_w.T + gate_b
        topk_val, topk_idx = jax.lax.top_k(logits, TOPK)
        probs = jax.nn.softmax(topk_val, axis=-1)
        out = jnp.zeros_like(xf)
        for kk in range(TOPK):
            idx = topk_idx[:, kk]
            w = probs[:, kk][:, None]
            for e in range(NE):
                mask = idx == e
                eo = _expert(xf, mask, ln1_w[e], ln1_b[e], in_proj_w[e], in_proj_b[e], out_proj_w[e], out_proj_b[e], ln2_w[e], ln2_b[e], mlp_w1[e], mlp_b1[e], mlp_w2[e], mlp_b2[e])
                out = out + jnp.where(mask[:, None], eo * w, 0.0)
        return out.reshape(B, N, E)
    edge_index = jnp.stack([src, dst])
    x = x + _L0_gnn_ref(_layernorm(x, axis=-1), edge_index, L0_gnn_W_l, L0_gnn_b_l, L0_gnn_W_r, L0_gnn_gamma, L0_gnn_beta)
    x = x + _L0_ffn_ref(_layernorm(x, axis=-1)[None], L0_ffn_gate_w, L0_ffn_gate_b, L0_ffn_ln1_w, L0_ffn_ln1_b, L0_ffn_in_proj_w, L0_ffn_in_proj_b, L0_ffn_out_proj_w, L0_ffn_out_proj_b, L0_ffn_ln2_w, L0_ffn_ln2_b, L0_ffn_mlp_w1, L0_ffn_mlp_b1, L0_ffn_mlp_w2, L0_ffn_mlp_b2)[0]
    return x

_drawn_inputs = setup_inputs


def setup_inputs(seed=0):
    import zlib

    import numpy as np

    out = dict(_drawn_inputs(seed))
    spreads = {'L0_gnn_b_l': (0.0, 2.0),
     'L0_gnn_gamma': (1.0, 0.2),
     'L0_gnn_beta': (0.0, 0.1),
     'L0_ffn_gate_b': (0.0, 0.376),
     'L0_ffn_ln1_w': (1.0, 0.6),
     'L0_ffn_ln1_b': (0.0, 0.8),
     'L0_ffn_in_proj_b': (0.0, 0.539),
     'L0_ffn_out_proj_b': (0.0, 0.529),
     'L0_ffn_ln2_w': (1.0, 0.6),
     'L0_ffn_ln2_b': (0.0, 2.0),
     'L0_ffn_mlp_b1': (0.0, 2.0),
     'L0_ffn_mlp_b2': (0.0, 0.54)}
    factors = {'L0_ffn_in_proj_w': 5.281, 'L0_ffn_out_proj_w': 3.118}
    for name, (base, spread) in spreads.items():
        noise = np.random.default_rng([zlib.crc32(name.encode()), seed]).standard_normal(out[name].shape)
        drawn = base * np.exp(spread * noise) if base else spread * noise
        out[name] = jnp.asarray(drawn.astype(out[name].dtype))
    for name, factor in factors.items():
        out[name] = (out[name] * factor).astype(out[name].dtype)
    return out
```

```python
from contextlib import ExitStack

import concourse.bass as bass
from concourse import mybir

F32 = mybir.dt.float32
F16 = mybir.dt.float16
I32 = mybir.dt.int32
ALU = mybir.AluOpType
ACT = mybir.ActivationFunctionType
AX = mybir.AxisListType

N = 1250
D = 512
P = 128
TT = 125
NT = N // TT
NB = 5
BW = N // NB
KC = D // P
E_EDGES = 20000
NCH = E_EDGES // TT
G = 8
NG = NCH // G
GS = 4
GH = G // 2
EPS = 1e-5
NE = 4
LB = 256
LW = NB * LB
BIG = 32768.0
LIST = 1536
H = 8
HD = D // H
HID = 256
NTL = LW // P
W_QKV = 0
W_OUT = KC * 3 * D
W_1 = W_OUT + KC * D
W_2 = W_1 + KC * HID
WCOLS = W_2 + HID // P * D
WP = 1024
NWP = WCOLS // WP
QKV_P, OUT_P, W1_P = (W_OUT - W_QKV) // WP, W_1 // WP, W_2 // WP
L1W, L1B, BQ, BK, BV, L2W, L2B, B1 = 0, 4, 8, 12, 16, 20, 24, 28
NPAR = 30
MARK = HD
SHIFT = 96
NPB = 4
FAR = -30000.0


class Tally:

    def __init__(self, engine, name, start=0):
        self.engine = engine
        self.reg = engine.alloc_register(name)
        engine.reg_mov(self.reg, start)
        self.off = 0

    def at(self, k):
        return self.engine.snap(self.reg) + (self.off + k)

    def skip(self, n):
        self.off += n

    def settle(self):
        if self.off:
            self.engine.reg_add(self.reg, self.reg, self.off)
        self.off = 0


def spans_of(nb):
    return [(c0, min(512, nb * LB - c0)) for c0 in range(0, nb * LB, 512)]


def settle(self):
        if self.off:
            self.engine.reg_add(self.reg, self.reg, self.off)
        self.off = 0


def settle(tallies):
    for t in tallies:
        t.settle()


def program(nc, x, src, dst, gnn_w, gnn_par, gate_w, gate_b, ew, epar_d, erow, out):
    stack = ExitStack()
    with stack:
        def sem(name):
            return stack.enter_context(nc.semaphore(name))

        def sb(name, shape, dt, where=None):
            return (where or stack).enter_context(nc.sbuf_tensor(name, shape, dt))

        def dram(name, shape, dt):
            return nc.dram_tensor(name, shape, dt, kind="Internal").ap()

        marks_dram = dram("marks_dram", (NE, 2, 2, LW), F16)
        es = dram("es", (NE * LIST, D), F32)
        x2_dram = dram("x2_dram", (N, D), F32)
        lists = dram("lists", (NE * LIST, 2 * D), F32)

        ident = sb("ident", [P, P], F32)
        nblocks = sb("nblocks", [1, NE], I32)
        slots = sb("slots", [TT, NT, 2], I32)
        probs = sb("probs", [TT, NT, 2], F32)
        x2_mem = sb("x2_mem", [P, NT * D], F32)
        x2 = x2_mem[0:TT, :].rearrange("p (t d) -> p t d", t=NT)
        w_raw = x2_mem[:, 0:2 * KC * D]
        banks = [stack.enter_context(nc.psum_tensor(f"bank{i}", [P, 512], F32)) for i in range(8)]

        gnn = ExitStack()
        big = sb("big", [P, NT * D], F32, gnn)
        xn = big[0:TT, :].rearrange("p (t d) -> p t d", t=NT)
        h_gnn = big[:, 0:KC * N].rearrange("p (c n) -> p c n", c=KC)
        xn_hi = sb("xn_hi", [TT, NT, D], F16, gnn)
        xn_lo = sb("xn_lo", [TT, NT, D], F16, gnn)
        xnT_hi = sb("xnT_hi", [P, KC, N], F16, gnn)
        xnT_lo = sb("xnT_lo", [P, KC, N], F16, gnn)
        at_hi = sb("at_hi", [TT, NT, N], F16, gnn)
        at_lo = sb("at_lo", [TT, NT, N], F16, gnn)
        onehot = sb("onehot", [P, 2 * KC * N], F16, gnn)
        oh_src = onehot[0:TT, :].rearrange("p (v g n) -> p v g n", v=2, g=GH)
        agg = onehot[:, :].rearrange("p (h c n) -> p h c n", h=2, c=KC)
        oh_dst = sb("oh_dst", [TT, 2, GH, TT], F16, gnn)
        iota = sb("iota", [TT, N], F16, gnn)
        edge_i = sb("edge_i", [TT, 2, NCH], I32, gnn)
        edge = sb("edge", [TT, 2, NCH], F32, gnn)
        a_row = sb("a_row", [TT, 2, N], F32, gnn)
        w_hi = sb("w_hi", [P, 2, KC, D], F16, gnn)
        w_lo = sb("w_lo", [P, 2, KC, D], F16, gnn)
        par = sb("par", [P, 3, KC], F32, gnn)
        span = sb("span", [P, 2, NG], F32, gnn)
        span_all = sb("span_all", [P, 2, NG], F32, gnn)
        tile0 = sb("tile0", [1, NT, NG], F32, gnn)
        meet_f = sb("meet_f", [1, 2, NT, NG], F32, gnn)
        meets = sb("meets", [1, 2, NT], I32, gnn)
        edge_to = sb("edge_to", [1, 2, NT], F32, gnn)
        g1 = sb("g1", [1, NG], F32, gnn)
        ones_h = sb("ones_h", [TT, P], F16, gnn)
        zrow = sb("zrow", [1, 640], F16, gnn)
        st6 = sb("st6", [P, NT, 6], F32, gnn)
        mv = sb("mv", [P, NT, 2], F32, gnn)
        half = sb("half", [P, NT], F32, gnn)
        rstd = sb("rstd", [P, NT], F32, gnn)
        bn6 = sb("bn6", [P, KC, NB, 6], F32, gnn)
        bnmv = sb("bnmv", [P, KC, 2], F32, gnn)
        bnr = sb("bnr", [P, KC], F32, gnn)
        scale = sb("scale", [P, KC], F32, gnn)
        shift = sb("shift", [P, KC], F32, gnn)
        rc = sb("rc", [P, 2, BW], F32, gnn)
        agg_f = sb("agg_f", [P, 2, BW], F32, gnn)
        x_again = sb("x_again", [TT, 2, D], F32, gnn)
        gnn.close()

        w_stage = sb("w_stage", [P, 2, WP], F32)
        w16 = sb("w16", [P, 2, WCOLS], F16)
        route = ExitStack()
        rows = sb("rows", [TT, NT, 2 * D], F32, route)
        gate = sb("gate", [TT, NE * D], F32, route)
        gate_bias = sb("gate_bias", [TT, NE], F32, route)
        prod = sb("prod", [TT, 2, D], F32, route)
        rst6 = sb("rst6", [TT, NT, 6], F32, route)
        rmv = sb("rmv", [TT, NT, 2], F32, route)
        rrstd = sb("rrstd", [TT, NT], F32, route)
        minus_half = sb("minus_half", [TT, NT], F32, route)
        logit = sb("logit", [TT, NE, NT], F32, route)
        beats = sb("beats", [TT, NE, NT, NE], F32, route)
        rank = sb("rank", [TT, NE, NT], F32, route)
        member = sb("member", [TT, 2, NE, NT], F32, route)
        member_h = sb("member_h", [TT, 2, NE, NT], F16, route)
        masked = sb("masked", [TT, 2, NE, NT], F32, route)
        best = sb("best", [TT, 2, NT], F32, route)
        gap = sb("gap", [TT, 4, NT], F32, route)
        tri = sb("tri", [TT, TT], F16, route)
        ones_r = sb("ones_r", [TT, P], F16, route)
        before = sb("before", [TT, 2, NE, NT], F32, route)
        tile_sum = sb("tile_sum", [P, 2, NE, NT], F32, route)
        tile_base = sb("tile_base", [P, 2, NE, NT + 1], F32, route)
        list0 = sb("list0", [TT, NE, NT], F32, route)
        slot_f = sb("slot_f", [TT, 2, NT], F32, route)
        total = sb("total", [P, NE], F32, route)
        pad_f = sb("pad_f", [P, NE, 2], F32, route)
        pad_row = sb("pad_row", [P, NE, 2], I32, route)
        pad_iota = sb("pad_iota", [P, NE, 2], F32, route)
        zeros = sb("zeros", [P, 2 * D], F32, route)
        blocks_f = sb("blocks_f", [1, 2, NE], F32, route)
        pos = sb("pos", [NE, LW], F32, route)
        own = sb("own", [NE, 2, NE], F32, route)
        bound = sb("bound", [NE, 2], F32, route)
        in_grp = sb("in_grp", [NE, 2, LW], F32, route)
        marks = sb("marks", [NE, 2, 2, LW], F16, route)
        route.close()

        ident_h = sb("ident_h", [P, P], F16)
        epar = sb("epar", [P, NE, NPAR], F32)
        ep = sb("ep", [P, NPAR], F32)
        ep_pair = sb("ep_pair", [P, 3], F32)
        hT = [sb(f"hT{i}", [P, KC, LW], F16) for i in range(2)]
        q_hi = sb("q_hi", [P, 2, LW], F16)
        k_hi = sb("k_hi", [P, 2, LW], F16)
        q_both = sb("q_both", [P, 2, LW], F16)
        k_both = sb("k_both", [P, 2, LW], F16)
        hid = [q_both, k_both]
        v_rows = x2_mem[:, :].rearrange("p (t d) -> p t d", t=NTL)
        v_head = sb("v_head", [P, 2, NTL, P], F32)
        probs_t = sb("probs_t", [P, NPB, 512], F32)
        oT = [sb(f"oT{i}", [P, H // 2, LW], F16) for i in range(2)]
        n2 = sb("n2", [P, 2, D], F32)
        t32 = sb("t32", [P, 2, 512], F32)
        halves = sb("halves", [P, 2, 2, 512], F16)
        row_par = sb("row_par", [P, 2, D], F32)
        rcp = sb("rcp", [HD, 2, 512], F32)
        o_tmp = sb("o_tmp", [P, 2, 512], F32)
        zero_row = sb("zero_row", [P, D], F32)
        mx = sb("mx", [P, 2, NTL, 3], F32)
        neg_max = sb("neg_max", [P, 2, NTL], F16)
        l2st = sb("l2st", [P, NTL, 6], F32)
        l2mv = sb("l2mv", [P, NTL, 2], F32)
        l2half = sb("l2half", [P, NTL], F32)
        l2r = sb("l2r", [P, NTL], F32)
        pp, sbk, stb, pvb = banks[0:2], banks[2:4], banks[4:6], banks[6:8]

        s_x = [sem(f"s_xin{t}") for t in range(NT)]
        s_edges = sem("s_edges")
        s_gw = sem("s_gw")
        s_par = sem("s_par")
        s_id = sem("s_id")
        s_const = sem("s_const")
        s_mv = sem("s_mv")
        s_rstd = sem("s_rstd")
        s_xn = sem("s_xn")
        s_xhi = sem("s_xhi")
        s_xlo = sem("s_xlo")
        s_whi = sem("s_whi")
        s_wlo = sem("s_wlo")
        s_xt = sem("s_xt")
        s_xthi = sem("s_xthi")
        s_xtlo = sem("s_xtlo")
        s_edge_f = sem("s_edge_f")
        s_span = sem("s_span")
        s_span_all = sem("s_span_all")
        s_meets = sem("s_meets")
        s_dch = sem("s_dch")
        s_oh = [sem(f"s_oh{v}") for v in range(2)]
        s_ohused = [sem(f"s_ohused{v}") for v in range(2)]
        s_arow = sem("s_arow")
        s_acopy = sem("s_acopy")
        s_at = sem("s_at")
        s_athi = sem("s_athi")
        s_atlo = sem("s_atlo")
        s_cnt = sem("s_cnt")
        s_rc = sem("s_rc")
        s_sum = sem("s_sum")
        s_aggf = sem("s_aggf")
        s_agghi = sem("s_agghi")
        s_agglo = sem("s_agglo")
        s_rc0 = sem("s_rc0")
        s_st = sem("s_st")
        s_bn6 = sem("s_bn6")
        s_h = sem("s_h")
        s_hT = sem("s_hT")
        s_bn = sem("s_bn")
        s_bnr = sem("s_bnr")
        s_scale = sem("s_scale")
        s_relu = sem("s_relu")
        s_back = sem("s_back")
        s_xagain = [sem(f"s_xagain{i}") for i in range(2)]
        s_x2 = sem("s_x2")
        s_x2out = sem("s_x2out")
        s_pch = sem("s_pch")
        s_routed = sem("s_routed")
        s_epar = sem("s_epar")
        s_ep = sem("s_ep")
        s_pair = sem("s_pair")
        s_idle = sem("s_idle")
        s_ech = sem("s_ech")
        s_wst = [sem(f"s_wst{i}") for i in range(2)]
        s_ehi = sem("s_ehi")
        s_elo = sem("s_elo")
        s_mk = sem("s_mk")
        s_rp = sem("s_rp")
        s_nr = [sem(f"s_nr{b}") for b in range(NB)]
        s_xr = sem("s_xr")
        s_es = sem("s_es")
        s_esz = sem("s_esz")
        s_stored = sem("s_stored")
        s_econst = sem("s_econst")
        s_pp = sem("s_pp")
        s_taken = sem("s_taken")
        s_split = sem("s_split")
        s_qkd = sem("s_qkd")
        s_qkp = sem("s_qkp")
        s_vh = sem("s_vh")
        s_s = sem("s_s")
        s_mx = sem("s_mx")
        s_neg = sem("s_neg")
        s_sT = sem("s_sT")
        s_exp = sem("s_exp")
        s_pv = sem("s_pv")
        s_on = sem("s_on")
        s_oT = sem("s_oT")
        s_xb = sem("s_xb")
        s_l2v = sem("s_l2v")
        s_l2r = sem("s_l2r")
        s_n2 = sem("s_n2")
        s_fin = sem("s_fin")
        s_g = [sem(f"s_g{i}") for i in range(2)]
        s_xy = [sem(f"s_xy{i}") for i in range(2)]
        s_y = sem("s_y")
        s_yout = [sem(f"s_yout{i}") for i in range(2)]
        s_gate = sem("s_gate")
        s_b = sem("s_b")
        s_rmv = sem("s_rmv")
        s_rr = sem("s_rr")
        s_xf = sem("s_xf")
        s_rn = sem("s_rn")
        s_rst = sem("s_rst")
        s_tri = sem("s_tri")
        s_rch = sem("s_rch")
        s_gap = sem("s_gap")
        s_ex = sem("s_ex")
        s_member = sem("s_member")
        s_pref = sem("s_pref")
        s_tot = sem("s_tot")
        s_slots = sem("s_slots")
        s_pads = sem("s_pads")
        s_marks = sem("s_marks")
        s_marksout = sem("s_marksout")
        s_scat = sem("s_scat")
        s_nblocks = sem("s_nblocks")
        s_zero = sem("s_zero")
        s_rpch = sem("s_rpch")
        s_logit = sem("s_logit")
        s_bound = sem("s_bound")

        w_r = w_raw.rearrange("p (m c n) -> p m c n", m=2, c=KC)
        x_t = x.rearrange("(t p) d -> p t d", p=TT)
        x2d_t = x2_dram.rearrange("(t p) d -> p t d", p=TT)
        b_at = [banks[6], banks[7]]
        ab = [banks[0:3], banks[3:6]]
        A_COLS = [(0, 512), (512, 512), (1024, N - 1024)]
        AT_COLS = [(0, 4), (4, 4), (8, 2)]

        block = stack.enter_context(nc.Block())

        @block.sync
        def _(sp):
            def load_piece(e, p):
                if isinstance(e, int):
                    if p >= 2:
                        sp.wait_ge(s_elo, p - 1)
                    rows_of_e = ew[e:e + 1, :, :]
                else:
                    rows_of_e = ew[bass.ds(nc.s_assert_within(e, 0, NE - 1), 1), :, :]
                    sp.wait_ge(s_elo, e * NWP + (p - 1))
                sp.dma_start(w_stage[:, p % 2, :], rows_of_e[:, :, p * WP:(p + 1) * WP].rearrange(
                    "a p n -> (a p) n")).then_inc(s_wst[p % 2], 16)

            sp.dma_start(edge_i[:, 0, :], src).then_inc(s_edges, 16)
            sp.dma_start(edge_i[:, 1, :], dst).then_inc(s_edges, 16)
            for t in range(NT):
                sp.dma_start(xn[:, t, :], x_t[:, t, :]).then_inc(s_x[t], 16)
            sp.dma_start(w_raw, gnn_w).then_inc(s_gw, 16)
            sp.dma_start(par[:, :, :], gnn_par).then_inc(s_par, 16)
            for t in range(NT):
                if t >= 2:
                    sp.wait_ge(s_x2, t - 1)
                sp.dma_start(x_again[:, t % 2, :], x_t[:, t, :]).then_inc(s_xagain[t % 2], 16)
            for t in range(NT):
                sp.wait_ge(s_x2, t + 1)
                sp.dma_start(x2d_t[:, t, :], x2[:, t, :]).then_inc(s_x2out, 16)
            sp.dma_start(gate[:, :], gate_w.partition_broadcast(TT)).then_inc(s_gate, 16)
            sp.dma_start(gate_bias[:, :], gate_b.partition_broadcast(TT)).then_inc(s_gate, 16)
            for p in range(QKV_P):
                load_piece(0, p)
            sp.wait_ge(s_marks, 1)
            sp.dma_start(marks_dram, marks[:, :, :, :]).then_inc(s_marksout, 16)
            sp.wait_ge(s_x2out, 16 * NT)
            sp.wait_ge(s_marksout, 16)
            sp.wait_ge(s_scat, 16 * (2 * NT + 2 * NE))
            sp.sem_inc(s_routed, 1)

            sp.sem_inc(s_es, 16)
            sp.dma_start(epar[:, :, :], epar_d).then_inc(s_epar, 16)
            sp.wait_ge(s_nblocks, 1)
            sp.wait_ge(s_econst, 9)

            def expert_sp(e, nb):
                for b in range(nb):
                    sp.dma_start(v_rows[:, 2 * b:2 * b + 2, :],
                                 lists[bass.ds(e * LIST + b * LB, LB), D:2 * D].rearrange("(t p) d -> p t d", p=P)
                                 ).then_inc(s_nr[b], 16)
                for side, m in enumerate((q_hi, k_hi)):
                    for hd in range(2):
                        sp.dma_start(m[MARK:MARK + 2, hd, :], marks_dram[bass.ds(e, 1), side, :, :].rearrange(
                            "a r n -> (a r) n")).then_inc(s_mk, 16)
                sp.dma_start(row_par[:, :, :], erow[bass.ds(e, 1), :, :].partition_broadcast(P)).then_inc(s_rp, 16)
                sp.dma_start(es[bass.ds(e * LIST + nb * LB, LIST - nb * LB), :].rearrange("(i p) d -> p i d", p=P),
                             zero_row[:, :].unsqueeze(1).broadcast_to([P, (LIST - nb * LB) // P, D])
                             ).then_inc(s_esz, 16)
                for p in range(QKV_P, NWP):
                    load_piece(e, p)
                with sp.If(e < NE - 1):
                    for p in range(2):
                        load_piece(e + 1, p)
                list_rows = lists[bass.ds(e * LIST, nb * LB), 0:D].rearrange("(t p) d -> p t d", p=P)
                sp.wait_ge(s_vh, e * H + H)
                sp.sem_inc(s_idle, 1)
                sp.dma_start(v_rows[:, 0:2 * nb, :], list_rows).then_inc(s_xr, 16)
                with sp.If(e < NE - 1):
                    for p in range(2, QKV_P):
                        load_piece(e + 1, p)
                es_rows = es[bass.ds(e * LIST, nb * LB), :].rearrange("(t p) d -> p t d", p=P)
                sp.wait_ge(s_fin, e + 2)
                sp.dma_start(es_rows, v_rows[:, 0:2 * nb, :]).then_inc(s_es, 16)

            with sp.Fori(0, NE) as e:
                sp.wait_ge(s_es, 16 * e + 16)
                nb_e = sp.value_load(nblocks[0:1, bass.ds(e, 1)], min_val=1, max_val=NB)
                for nb in range(1, NB + 1):
                    with sp.If(nb_e == nb):
                        expert_sp(e, nb)
            sp.wait_ge(s_es, 16 * NE + 16)
            sp.wait_ge(s_esz, 16 * NE)
            sp.sem_inc(s_stored, 1)

            def x2_again(t):
                sp.dma_start(t32[0:TT, t % 2, :], x2d_t[:, t, :]).then_inc(s_xy[t % 2], 16)

            x2_again(0)
            x2_again(1)
            for t in range(NT):
                sp.wait_ge(s_y, t + 1)
                sp.dma_start(out.rearrange("(t p) d -> p t d", p=TT)[:, t, :], n2[0:TT, t % 2, :]
                             ).then_inc(s_yout[t % 2], 16)
                if t + 2 < NT:
                    x2_again(t + 2)
            for i in range(2):
                sp.wait_ge(s_yout[i], 16 * (NT // 2))

        @block.gpsimd
        def _(pool):
            def low_weights(e, p):
                cols = slice(p * WP, (p + 1) * WP)
                pool.wait_ge(s_ehi, e * NWP + (p + 1))
                nc.gpsimd.tensor_tensor(w16[:, 1, cols], w_stage[:, p % 2, :], w16[:, 0, cols],
                                        ALU.subtract).then_inc(s_elo, 1)

            nc.gpsimd.memset(ident[:, :], 0.0).then_inc(s_pch, 1)
            nc.gpsimd.memset(half[:, :], -0.5).then_inc(s_pch, 1)
            nc.gpsimd.memset(ones_h[:, :], 1.0).then_inc(s_const, 1)
            nc.gpsimd.memset(zrow[:, :], 0.0).then_inc(s_const, 1)
            nc.gpsimd.iota(iota[:, :], pattern=[[1, N]], base=0, channel_multiplier=0,
                           allow_small_or_imprecise_dtypes=True).then_inc(s_const, 1)
            nc.gpsimd.iota(tile0[:, :, :], pattern=[[TT, NT], [0, NG]], base=0, channel_multiplier=0,
                           allow_small_or_imprecise_dtypes=True).then_inc(s_const, 1)
            nc.gpsimd.iota(g1[:, :], pattern=[[1, NG]], base=1, channel_multiplier=0,
                           allow_small_or_imprecise_dtypes=True).then_inc(s_const, 1)
            pool.wait_ge(s_pch, 2)
            nc.gpsimd.affine_select(out=ident[:, :], in_=ident[:, :], compare_op=ALU.not_equal, fill=1.0,
                                    base=0, pattern=[[-1, P]], channel_multiplier=1).then_inc(s_id, 1)
            pool.wait_ge(s_span, 1)
            for k in range(2):
                nc.gpsimd.partition_all_reduce(span_all[:, k, :], span[:, k, :], P,
                                               bass.bass_isa.ReduceOp.max).then_inc(s_span_all, 1)
            pool.wait_ge(s_mv, 1)
            nc.gpsimd.tensor_tensor(rstd[0:TT, :], mv[0:TT, :, 1], half[0:TT, :], ALU.pow).then_inc(s_rstd, 1)
            for t in range(NT):
                pool.wait_ge(s_xhi, t + 1)
                nc.gpsimd.tensor_tensor(xn_lo[:, t, :], xn[:, t, :], xn_hi[:, t, :], ALU.subtract).then_inc(s_xlo, 1)
            for m in range(2):
                pool.wait_ge(s_whi, m + 1)
                nc.gpsimd.tensor_tensor(w_lo[:, m, :, :], w_r[:, m, :, :], w_hi[:, m, :, :],
                                        ALU.subtract).then_inc(s_wlo, 1)
            pool.sem_inc(s_agglo, 2)
            with nc.gpsimd.Fori(0, NB) as b:
                for c in range(KC):
                    pool.wait_ge(s_agghi, b * KC + (c + 1))
                    nc.gpsimd.tensor_tensor(agg[:, 1, c, bass.ds(b * BW, BW)], agg_f[:, c % 2, :],
                                            agg[:, 0, c, bass.ds(b * BW, BW)], ALU.subtract).then_inc(s_agglo, 1)
            pool.wait_ge(s_bn, 1)
            nc.gpsimd.tensor_tensor(bnr[:, :], bnmv[:, :, 1], half[:, 0:KC], ALU.pow).then_inc(s_bnr, 1)

            pool.wait_ge(s_x2, NT)
            nc.gpsimd.memset(minus_half[:, :], -0.5).then_inc(s_rpch, 1)
            nc.gpsimd.memset(tri[:, :], 1.0).then_inc(s_rpch, 1)
            nc.gpsimd.memset(ones_r[:, :], 1.0).then_inc(s_tri, 1)
            nc.gpsimd.iota(list0[:, :, :], pattern=[[LIST, NE], [0, NT]], base=0, channel_multiplier=0,
                           allow_small_or_imprecise_dtypes=True).then_inc(s_tri, 1)
            nc.gpsimd.iota(pad_iota[:, :, :], pattern=[[LIST, NE], [P, 2]], base=0, channel_multiplier=1,
                           allow_small_or_imprecise_dtypes=True).then_inc(s_tri, 1)
            nc.gpsimd.iota(pos[:, :], pattern=[[1, LW]], base=0, channel_multiplier=0,
                           allow_small_or_imprecise_dtypes=True).then_inc(s_tri, 1)
            pool.wait_ge(s_rpch, 2)
            nc.gpsimd.affine_select(out=tri[:, :], in_=tri[:, :], compare_op=ALU.is_gt, fill=0.0,
                                    base=0, pattern=[[1, TT]], channel_multiplier=-1).then_inc(s_tri, 1)
            pool.wait_ge(s_rmv, 1)
            nc.gpsimd.tensor_tensor(rrstd[:, :], rmv[:, :, 1], minus_half[:, :], ALU.pow).then_inc(s_rr, 1)
            nc.gpsimd.memset(zeros[:, :], 0.0).then_inc(s_zero, 1)
            pool.wait_ge(s_rmv, 2)
            nc.gpsimd.tensor_tensor(rrstd[:, :], rmv[:, :, 1], minus_half[:, :], ALU.pow).then_inc(s_rr, 1)
            for p in range(QKV_P):
                low_weights(0, p)
            pool.wait_ge(s_slots, 1)
            pool.wait_ge(s_rn, NT)
            for t in range(NT):
                for k in range(2):
                    nc.gpsimd.indirect_dma_start(
                        out=lists, out_offset=bass.IndirectOffsetOnAxis(ap=slots[:, t, k:k + 1], axis=0),
                        in_=rows[:, t, :], in_offset=None, bounds_check=NE * LIST - 1,
                        oob_is_err=False).then_inc(s_scat, 16)
            pool.wait_ge(s_zero, 1)
            pool.wait_ge(s_pads, 1)
            for e in range(NE):
                for i in range(2):
                    nc.gpsimd.indirect_dma_start(
                        out=lists, out_offset=bass.IndirectOffsetOnAxis(ap=pad_row[:, e, i:i + 1], axis=0),
                        in_=zeros[:, :], in_offset=None, bounds_check=NE * LIST - 1,
                        oob_is_err=False).then_inc(s_scat, 16)

            pool.wait_ge(s_routed, 1)
            nc.gpsimd.tensor_copy(ident_h[:, :], ident[:, :]).then_inc(s_econst, 1)
            nc.gpsimd.memset(q_hi[:, :, :], 0.0).then_inc(s_econst, 1)
            nc.gpsimd.memset(k_hi[:, :, :], 0.0).then_inc(s_econst, 1)
            nc.gpsimd.memset(v_head[:, :, :, HD:P], 1.0).then_inc(s_econst, 1)
            nc.gpsimd.memset(l2half[:, :], -0.5).then_inc(s_econst, 1)
            nc.gpsimd.memset(zero_row[:, :], 0.0).then_inc(s_econst, 1)
            pool.wait_ge(s_econst, 6)
            nc.gpsimd.memset(k_hi[SHIFT:SHIFT + 1, :, :], 1.0).then_inc(s_econst, 3)
            pool.wait_ge(s_econst, 9)
            taken = Tally(pool, "pool_taken", 2)
            split = Tally(pool, "pool_split", 2)
            scored = Tally(pool, "pool_scored", 1)
            summed = Tally(pool, "pool_summed", 4)
            biased = Tally(pool, "pool_biased", 0)
            normed = Tally(pool, "pool_normed", 0)
            pool.sem_inc(s_qkp, 2)

            def expert_pool(e, nb):
                spans, nt = spans_of(nb), 2 * nb
                ns = len(spans)
                for p in range(QKV_P, NWP):
                    low_weights(e, p)
                taken.skip(2 * nt)
                split.skip(nt)
                pool.wait_ge(s_taken, taken.at(0))
                for r in (taken, split):
                    r.settle()
                with nc.gpsimd.Fori(0, H // 2) as j:
                    pool.wait_ge(s_pv, summed.at(0))
                    pool.sem_inc(s_idle, 1)
                    for hd in range(2):
                        nc.gpsimd.tensor_copy(v_head[:, hd, 0:nt, 0:HD],
                                              v_rows[:, 0:nt, bass.ds(j * P + hd * HD, HD)]).then_inc(s_vh, 1)
                    pool.wait_ge(s_sT, scored.at(0))
                    for s, (c0, cn) in enumerate(spans):
                        for side in range(2):
                            r = side
                            cols = slice(c0, c0 + cn)
                            pool.wait_ge(s_split, split.at(2 * s + side + 1))
                            pool.sem_inc(s_idle, 1)
                            high, low = halves[:, r, 0, 0:cn], halves[:, r, 1, 0:cn]
                            if side == 0:
                                nc.gpsimd.tensor_copy(q_hi[0:HD, 0, cols], high[0:HD])
                                last = nc.gpsimd.tensor_copy(q_both[0:HD, 0, cols], high[0:HD])
                            else:
                                nc.gpsimd.tensor_copy(k_hi[0:HD, 0, cols], high[0:HD])
                                last = nc.gpsimd.tensor_copy(k_both[0:HD, 0, cols], low[0:HD])
                            last.then_inc(s_qkp, 1)
                    split.skip(2 * ns)
                    scored.skip(2 * ns * nt)
                    summed.skip(2 * ns * nt)
                    for r in (split, scored, summed):
                        r.settle()
                pool.wait_ge(s_xr, e * 16 + 16)
                pool.wait_ge(s_rp, e * 16 + 16)
                for t in range(nt):
                    nc.gpsimd.tensor_tensor(v_rows[:, t, :], v_rows[:, t, :], row_par[:, 0, :],
                                            ALU.add).then_inc(s_xb, 1)
                pool.wait_ge(s_l2v, e + 1)
                nc.gpsimd.tensor_tensor(l2r[:, 0:nt], l2mv[:, 0:nt, 1], l2half[:, 0:nt], ALU.pow).then_inc(s_l2r, 1)
                for t in range(nt):
                    pool.wait_ge(s_n2, normed.at(t + 1))
                    nc.gpsimd.tensor_tensor(v_rows[:, t, :], v_rows[:, t, :], row_par[:, 1, :],
                                            ALU.add).then_inc(s_xb, 1)
                with nc.gpsimd.If(e < NE - 1):
                    for p in range(QKV_P):
                        low_weights(e + 1, p)
                normed.skip(nt)
                taken.skip(8 * ns * 2 + 3 * nt + 2 * ns)
                split.skip(nt + 2 * ns)
                for r in (taken, split, normed):
                    r.settle()

            with nc.gpsimd.Fori(0, NE) as e:
                nb_e = nc.gpsimd.value_load(nblocks[0:1, bass.ds(e, 1)], min_val=1, max_val=NB)
                for nb in range(1, NB + 1):
                    with nc.gpsimd.If(nb_e == nb):
                        expert_pool(e, nb)

            pool.wait_ge(s_stored, 1)
            for t in range(NT):
                if t >= 2:
                    pool.wait_ge(s_y, t - 1)
                for k in range(2):
                    nc.gpsimd.indirect_dma_start(
                        out=probs_t[0:TT, 2 * (t % 2) + k, :], out_offset=None, in_=es,
                        in_offset=bass.IndirectOffsetOnAxis(ap=slots[:, t, k:k + 1], axis=0),
                        bounds_check=NE * LIST - 1, oob_is_err=False).then_inc(s_g[t % 2], 16)

        @block.scalar
        def _(act):
            def high_weights(e, p):
                act.wait_ge(s_wst[p % 2], e * (16 * NWP // 2) + 16 * (p // 2 + 1))
                nc.scalar.copy(w16[:, 0, p * WP:(p + 1) * WP], w_stage[:, p % 2, :]).then_inc(s_ehi, 1)

            act.sem_inc(s_acopy, 2)
            act.sem_inc(s_hT, 2)
            for t in range(NT):
                act.wait_ge(s_xn, t + 1)
                nc.scalar.copy(xn_hi[:, t, :], xn[:, t, :]).then_inc(s_xhi, 1)
            for t in range(NT):
                act.wait_ge(s_xt, t + 1)
                nc.scalar.copy(xnT_hi[:, :, t * TT:(t + 1) * TT],
                               banks[6 + t % 2][:, 0:KC * TT].rearrange("p (c n) -> p c n", c=KC)).then_inc(s_xthi, 1)
            act.wait_ge(s_gw, 16)
            for m in range(2):
                nc.scalar.copy(w_hi[:, m, :, :], w_r[:, m, :, :]).then_inc(s_whi, 1)

            def copy_rows(t, u):
                act.wait_ge(s_arow, t + 1)
                for k, (c0, cn) in enumerate(A_COLS):
                    last = nc.scalar.copy(a_row[:, u, c0:c0 + cn], ab[u][k][0:TT, 0:cn])
                last.then_inc(s_acopy, 1)

            def high_counts(t, u):
                for k, (s0, sn) in enumerate(AT_COLS):
                    act.wait_ge(s_at, t * 3 + (k + 1))
                    nc.scalar.copy(at_hi[:, s0:s0 + sn, bass.ds(t * TT, TT)],
                                   b_at[(3 * u + k) % 2][0:TT, 0:sn * TT].rearrange("p (s n) -> p s n", s=sn)
                                   ).then_inc(s_athi, 1)

            copy_rows(0, 0)
            with nc.scalar.Fori(0, NT // 2 - 1) as tt:
                for u in range(2):
                    copy_rows(tt * 2 + u + 1, 1 - u)
                    high_counts(tt * 2 + u, u)
            copy_rows(NT - 1, 1)
            high_counts(NT - 2, 0)
            high_counts(NT - 1, 1)
            with nc.scalar.Fori(0, NB) as b:
                for c in range(KC):
                    act.wait_ge(s_aggf, b * KC + (c + 3))
                    nc.scalar.copy(agg[:, 0, c, bass.ds(b * BW, BW)], agg_f[:, c % 2, :]).then_inc(s_agghi, 1)
            act.wait_ge(s_par, 16)
            with nc.scalar.Fori(0, NB) as b:
                for c in range(KC):
                    act.wait_ge(s_h, b * KC + (c + 1))
                    nc.scalar.activation(h_gnn[:, c, bass.ds(b * BW, BW)], banks[c % 2][:, 0:BW], ACT.Identity,
                                         bias=par[:, 0, c:c + 1]).then_inc(s_hT, 1)
            act.wait_ge(s_scale, 1)
            for c in range(KC):
                nc.scalar.activation(h_gnn[:, c, :], h_gnn[:, c, :], ACT.Relu, bias=shift[:, c:c + 1],
                                     scale=scale[:, c:c + 1]).then_inc(s_relu, 1)

            for p in range(QKV_P):
                high_weights(0, p)
            act.wait_ge(s_gap, 1)
            nc.scalar.activation(gap[:, 1, :], gap[:, 0, :], ACT.Exp).then_inc(s_ex, 1)

            act.wait_ge(s_nblocks, 1)
            act.wait_ge(s_routed, 1)
            act.wait_ge(s_econst, 9)
            act.sem_inc(s_taken, 2)
            act.sem_inc(s_exp, 2)
            filled = Tally(act, "act_filled", 0)
            split = Tally(act, "act_split", 2)
            scored = Tally(act, "act_scored", 1)
            summed = Tally(act, "act_summed", 4)

            def scaled_columns(nt, w0, b0):
                for t in range(nt):
                    act.wait_ge(s_pp, filled.at(t + 1))
                    act.wait_ge(s_split, split.at(t - 1))
                    for c in range(KC):
                        last = nc.scalar.activation(t32[:, t % 2, c * P:(c + 1) * P], pp[t % 2][:, c * P:(c + 1) * P],
                                                    ACT.Identity, bias=ep[:, b0 + c:b0 + c + 1],
                                                    scale=ep[:, w0 + c:w0 + c + 1])
                    last.then_inc(s_taken, 1)
                filled.skip(nt)
                split.skip(nt)

            def expert_act(e, nb):
                spans, nt = spans_of(nb), 2 * nb
                ns = len(spans)
                act.wait_ge(s_ep, e + 1)
                act.wait_ge(s_fin, e + 1)
                scaled_columns(nt, L1W, L1B)
                act.wait_ge(s_split, split.at(0))
                for t in range(nt):
                    act.wait_ge(s_pp, filled.at(t + 1))
                    nc.scalar.copy(v_rows[:, t, :], pp[t % 2][:, :]).then_inc(s_taken, 1)
                filled.skip(nt)
                for p in range(QKV_P, NWP):
                    high_weights(e, p)
                for r in (filled, split):
                    r.settle()
                with nc.scalar.Fori(0, H // 2) as j:
                    act.wait_ge(s_pair, e * (H // 2) + j + 1)
                    for k in range(2 * ns):
                        s, side = k // 2, k % 2
                        cn = spans[s][1]
                        act.wait_ge(s_pp, filled.at(k + 1))
                        act.wait_ge(s_split, split.at(k - 1))
                        nc.scalar.activation(t32[:, k % 2, 0:cn], pp[k % 2][:, 0:cn], ACT.Identity,
                                             bias=ep_pair[:, side:side + 1],
                                             scale=(HD ** -0.5, 1.0)[side]).then_inc(s_taken, 1)
                    filled.skip(2 * ns)
                    split.skip(2 * ns)
                    for hd in range(2):
                        for s, (c0, cn) in enumerate(spans):
                            act.wait_ge(s_pp, filled.at(s + 1))
                            nc.scalar.copy(q_hi[SHIFT:SHIFT + 1, hd, c0:c0 + cn],
                                           pp[(hd * ns + s) % 2][0:1, 0:cn]).then_inc(s_taken, 1)
                        filled.skip(ns)
                        for i in range(ns * nt):
                            x = hd * ns * nt + i
                            cn = spans[i // nt][1]
                            act.wait_ge(s_sT, scored.at(i + 1))
                            act.wait_ge(s_pv, summed.at(i - 3))
                            nc.scalar.activation(probs_t[:, x % NPB, 0:cn], stb[x % 2][:, 0:cn],
                                                 ACT.Exp).then_inc(s_exp, 1)
                        scored.skip(ns * nt)
                        summed.skip(ns * nt)
                    for r in (filled, split, scored, summed):
                        r.settle()
                filled.skip(nt)
                scaled_columns(nt, L2W, L2B)
                for k in range(2 * ns):
                    hc, s = k // ns, k % ns
                    cn = spans[s][1]
                    act.wait_ge(s_pp, filled.at(k + 1))
                    act.wait_ge(s_split, split.at(k - 1))
                    nc.scalar.activation(t32[:, k % 2, 0:cn], pp[k % 2][:, 0:cn], ACT.Gelu,
                                         bias=ep[:, B1 + hc:B1 + hc + 1]).then_inc(s_taken, 1)
                filled.skip(2 * ns)
                split.skip(2 * ns)
                with nc.scalar.If(e < NE - 1):
                    for p in range(QKV_P):
                        high_weights(e + 1, p)
                filled.skip(nt)
                for r in (filled, split, scored, summed):
                    r.settle()

            with nc.scalar.Fori(0, NE) as e:
                nb_e = nc.scalar.value_load(nblocks[0:1, bass.ds(e, 1)], min_val=1, max_val=NB)
                for nb in range(1, NB + 1):
                    with nc.scalar.If(nb_e == nb):
                        expert_act(e, nb)

        @block.tensor
        def _(pe):
            pe.wait_ge(s_id, 1)
            for t in range(NT):
                pe.wait_ge(s_xn, t + 1)
                if t >= 2:
                    pe.wait_ge(s_xtlo, t - 1)
                for c in range(KC):
                    last = nc.tensor.transpose(banks[6 + t % 2][:, c * TT:(c + 1) * TT],
                                               xn[:, t, c * P:(c + 1) * P], ident[0:TT, 0:TT])
                last.then_inc(s_xt, 1)
            pe.wait_ge(s_const, 5)
            pe.wait_ge(s_meets, 1)
            filled = pe.alloc_register("pe_filled")
            pe.reg_mov(filled, 1)

            def count_rows(t, u):
                pe.wait_ge(s_acopy, t + 1)
                for k, (c0, cn) in enumerate(A_COLS):
                    nc.tensor.matmul(ab[u][k][0:TT, 0:cn], zrow[0:1, 0:TT], zrow[0:1, 0:cn], start=True, stop=True,
                                     skip_group_check=True)
                first = nc.tensor.value_load(meets[0:1, 0, bass.ds(t, 1)], min_val=0, max_val=2 * NG)
                end = nc.tensor.value_load(meets[0:1, 1, bass.ds(t, 1)], min_val=0, max_val=NG)
                with nc.tensor.Fori(0, NG // GS) as gs:
                    with nc.tensor.If((gs * GS + GS > first) & (gs * GS < end)):
                        for gi in range(GS):
                            g = gs * GS + gi
                            with nc.tensor.If((g >= first) & (g < end)):
                                fill = nc.tensor.snap(filled)
                                for v in range(2):
                                    pe.wait_ge(s_oh[v], fill)
                                    for i in range(GH):
                                        for k, (c0, cn) in enumerate(A_COLS):
                                            last = nc.tensor.matmul(ab[u][k][0:TT, 0:cn], oh_dst[:, v, i, :],
                                                                    oh_src[:, v, i, c0:c0 + cn], start=False,
                                                                    stop=True, skip_group_check=True)
                                    last.then_inc(s_ohused[v], 1)
                                pe.reg_add(filled, filled, 1)
                nc.tensor.matmul(ab[u][0][0:TT, 0:1], zrow[0:1, 0:TT], zrow[0:1, 0:1], start=False, stop=True,
                                 skip_group_check=True).then_inc(s_arow, 1)

            def turn_rows(t, u):
                pe.wait_ge(s_acopy, t + 3)
                for k, (s0, sn) in enumerate(AT_COLS):
                    pe.wait_ge(s_atlo, t * 3 + (k + 1))
                    for s in range(sn):
                        last = nc.tensor.transpose(b_at[(3 * u + k) % 2][0:TT, s * TT:(s + 1) * TT],
                                                   a_row[:, u, (s0 + s) * TT:(s0 + s + 1) * TT], ident[0:TT, 0:TT])
                    last.then_inc(s_at, 1)

            pe.wait_ge(s_xtlo, NT)
            count_rows(0, 0)
            with nc.tensor.Fori(0, NT // 2 - 1) as tt:
                for u in range(2):
                    count_rows(tt * 2 + u + 1, 1 - u)
                    turn_rows(tt * 2 + u, u)
            count_rows(NT - 1, 1)
            turn_rows(NT - 2, 0)
            turn_rows(NT - 1, 1)

            pe.wait_ge(s_xlo, NT)
            pe.wait_ge(s_atlo, 3 * NT + 2)
            with nc.tensor.Fori(0, NB) as b:
                pe.wait_ge(s_rc, b + 1)
                for k, m in enumerate([at_hi, at_lo]):
                    for s in range(NT):
                        last = nc.tensor.matmul(banks[2][:, 0:BW], ones_h[:, :], m[:, s, bass.ds(b * BW, BW)],
                                                start=(k == 0 and s == 0), stop=(k == 1 and s == NT - 1))
                last.then_inc(s_cnt, 1)
                for c in range(KC):
                    pe.wait_ge(s_aggf, b * KC + (c + 1))
                    for k, (w, m) in enumerate([(xn_hi, at_hi), (xn_lo, at_hi), (xn_hi, at_lo)]):
                        for s in range(NT):
                            last = nc.tensor.matmul(banks[c % 2][:, 0:BW], w[:, s, c * P:(c + 1) * P],
                                                    m[:, s, bass.ds(b * BW, BW)],
                                                    start=(k == 0 and s == 0), stop=(k == 2 and s == NT - 1))
                    last.then_inc(s_sum, 1)
            pe.wait_ge(s_wlo, 2)
            pe.wait_ge(s_agglo, NB * KC + 2)
            with nc.tensor.Fori(0, NB) as b:
                for c in range(KC):
                    pe.wait_ge(s_hT, b * KC + (c + 1))
                    for m, (hi, lo) in enumerate([(agg[:, 0], agg[:, 1]), (xnT_hi, xnT_lo)]):
                        for k, (w, a) in enumerate([(w_hi, hi), (w_lo, hi), (w_hi, lo)]):
                            for j in range(KC):
                                last = nc.tensor.matmul(banks[c % 2][:, 0:BW], w[:, m, j, c * P:(c + 1) * P],
                                                        a[:, j, bass.ds(b * BW, BW)],
                                                        start=(m == 0 and k == 0 and j == 0),
                                                        stop=(m == 1 and k == 2 and j == KC - 1))
                    last.then_inc(s_h, 1)
            for t in range(NT):
                if t == 0:
                    pe.wait_ge(s_relu, KC)
                if t >= 2:
                    pe.wait_ge(s_x2, t - 1)
                for c in range(KC):
                    last = nc.tensor.transpose(banks[2 + t % 2][0:TT, c * P:(c + 1) * P],
                                               h_gnn[:, c, t * TT:(t + 1) * TT], ident[:, :])
                last.then_inc(s_back, 1)

            pe.wait_ge(s_member, 1)
            pe.wait_ge(s_tri, 5)
            members = member_h[:, :, :, :].rearrange("p k e t -> p (k e t)")
            nc.tensor.matmul(banks[0][0:TT, 0:2 * NE * NT], tri[:, :], members, start=True, stop=True).then_inc(s_pref, 1)
            nc.tensor.matmul(banks[1][:, 0:2 * NE * NT], ones_r[:, :], members, start=True, stop=True).then_inc(s_tot, 1)

            pe.wait_ge(s_nblocks, 1)
            pe.wait_ge(s_routed, 1)
            pe.wait_ge(s_econst, 9)
            pe.wait_ge(s_slots, 1)
            pe.sem_inc(s_sT, 1)
            pe.sem_inc(s_pv, 4)
            loaded = [Tally(pe, f"pe_loaded{b}", 0) for b in range(NB)]
            taken = Tally(pe, "pe_taken", 2)
            split = Tally(pe, "pe_split", 2)
            maxed = Tally(pe, "pe_maxed", 2)
            exped = Tally(pe, "pe_exped", 2)
            on = Tally(pe, "pe_on", 2)
            oT_done = Tally(pe, "pe_oT", 0)
            qkd = Tally(pe, "pe_qkd", 0)
            qkp = Tally(pe, "pe_qkp", 2)
            normed = Tally(pe, "pe_normed", 0)
            counts = loaded + [taken, split, maxed, exped, on, oT_done, qkd, qkp, normed]
            PASSES = [(0, 0), (1, 0), (0, 1)]

            def product(bank, lhs, rhs, chunks):
                for n, (a, b) in enumerate(PASSES):
                    for c in range(chunks):
                        last = nc.tensor.matmul(bank, lhs(a, c), rhs(b, c), start=(n == 0 and c == 0),
                                                stop=(n == 2 and c == chunks - 1))
                return last

            def turn(rows_of, t):
                for c in range(KC):
                    last = nc.tensor.transpose(pp[t % 2][:, c * P:(c + 1) * P], rows_of[:, c * P:(c + 1) * P],
                                               ident[:, :])
                last.then_inc(s_pp, 1)

            def expert_pe(e, nb):
                spans, nt = spans_of(nb), 2 * nb
                ns = len(spans)
                nx = ns * nt
                for t in range(nt):
                    if t % 2 == 0:
                        pe.wait_ge(s_nr[t // 2], loaded[t // 2].at(16))
                        loaded[t // 2].skip(16)
                    pe.wait_ge(s_taken, taken.at(t - 1))
                    turn(v_rows[:, t, :], t)
                taken.skip(nt)
                pe.wait_ge(s_elo, e * NWP + QKV_P)
                pe.wait_ge(s_split, split.at(nt))
                split.skip(nt)
                for t in range(nt):
                    pe.wait_ge(s_taken, taken.at(t - 1))
                    product(pp[t % 2][:, :], lambda a, c: hT[a][:, c, t * P:(t + 1) * P],
                            lambda b, c: w16[:, b, c * 3 * D + 2 * D:(c + 1) * 3 * D], KC).then_inc(s_pp, 1)
                taken.skip(nt)
                for r in counts:
                    r.settle()
                with nc.tensor.Fori(0, H // 2) as j:
                    for k in range(2 * ns):
                        s, side = k // 2, k % 2
                        c0, cn = spans[s]
                        pe.wait_ge(s_taken, taken.at(k - 1))
                        product(pp[k % 2][:, 0:cn],
                                lambda a, c: w16[:, a, bass.ds(j * P + (c * 3 * D + side * D), P)],
                                lambda b, c: hT[b][:, c, c0:c0 + cn], KC).then_inc(s_pp, 1)
                    taken.skip(2 * ns)
                    pe.wait_ge(s_qkd, qkd.at(2 * ns))
                    pe.wait_ge(s_qkp, qkp.at(2 * ns))
                    pe.wait_ge(s_mk, e * 64 + 64)
                    qkd.skip(2 * ns)
                    split.skip(2 * ns)
                    qkp.skip(2 * ns)

                    def scores(hd, i):
                        t, (c0, cn) = i // ns, spans[i % ns]
                        x = hd * nx + i
                        pe.wait_ge(s_mx, maxed.at(x - 1))
                        nc.tensor.matmul(sbk[x % 2][:, 0:cn], q_hi[0:MARK + 2, hd, t * P:(t + 1) * P],
                                         k_hi[0:MARK + 2, hd, c0:c0 + cn], start=True, stop=True).then_inc(s_s, 1)

                    def maxima_row(hd):
                        pe.wait_ge(s_neg, neg.at(hd + 1))
                        for s, (c0, cn) in enumerate(spans):
                            pe.wait_ge(s_taken, taken.at(s - 1))
                            for i in range(cn // P):
                                t = c0 // P + i
                                last = nc.tensor.matmul(pp[(hd * ns + s) % 2][0:1, i * P:(i + 1) * P],
                                                        neg_max[:, hd, t:t + 1], ident_h[:, :], start=True, stop=True)
                            last.then_inc(s_pp, 1)
                        taken.skip(ns)

                    def scores_t(hd, i):
                        s, kt = i // nt, i % nt
                        c0, cn = spans[s]
                        x = hd * nx + i
                        pe.wait_ge(s_exp, exped.at(x - 1))
                        if kt == 0:
                            pe.wait_ge(s_taken, taken.at(s + 1 - ns))
                        nc.tensor.matmul(stb[x % 2][:, 0:cn], k_hi[0:SHIFT + 1, hd, kt * P:(kt + 1) * P],
                                         q_hi[0:SHIFT + 1, hd, c0:c0 + cn], start=True, stop=False)
                        nc.tensor.matmul(stb[x % 2][:, 0:cn], k_both[:, hd, kt * P:(kt + 1) * P],
                                         q_both[:, hd, c0:c0 + cn], start=False, stop=True).then_inc(s_sT, 1)

                    def sums(hd, i):
                        s, kt = i // nt, i % nt
                        cn = spans[s][1]
                        x = hd * nx + i
                        copied, divided, made = e * H + j * 2 + (hd + 1), on.at(hd * ns + s - 1), exped.at(x + 1)
                        if i == 0:
                            pe.wait_ge(s_vh, copied)
                        if kt == 0:
                            pe.wait_ge(s_on, divided)
                        pe.wait_ge(s_exp, made)
                        nc.tensor.matmul(pvb[(hd * ns + s) % 2][:, 0:cn], v_head[:, hd, kt, :],
                                         probs_t[:, x % NPB, 0:cn], start=(kt == 0),
                                         stop=(kt == nt - 1)).then_inc(s_pv, 1)

                    for i in range(nx):
                        scores(0, i)
                    for hd in range(2):
                        maxima_row(hd)
                        scores_t(hd, 0)
                        scores_t(hd, 1)
                        for i in range(nx):
                            sums(hd, i)
                            if i + 2 < nx:
                                scores_t(hd, i + 2)
                            if hd == 0:
                                scores(1, i)
                    maxed.skip(2 * nx)
                    exped.skip(2 * nx)
                    on.skip(2 * ns)
                    oT_done.skip(2 * ns)
                    neg.skip(2)
                    for r in counts:
                        r.settle()
                heads, emptied, split_up = oT_done.at(0), taken.at(0), e * NWP + OUT_P
                pe.wait_ge(s_oT, heads)
                pe.wait_ge(s_taken, emptied)
                pe.wait_ge(s_elo, split_up)
                for t in range(nt):
                    pe.wait_ge(s_taken, taken.at(t - 1))
                    product(pp[t % 2][:, :], lambda a, c: oT[a][:, c, t * P:(t + 1) * P],
                            lambda b, c: w16[:, b, W_OUT + c * D:W_OUT + (c + 1) * D], KC).then_inc(s_pp, 1)
                taken.skip(nt)
                for t in range(nt):
                    pe.wait_ge(s_taken, taken.at(max(t - 1, 0)))
                    pe.wait_ge(s_n2, normed.at(t + 1))
                    turn(n2[:, t % 2, :], t)
                taken.skip(nt)
                normed.skip(nt)
                pe.wait_ge(s_elo, e * NWP + W1_P)
                pe.wait_ge(s_split, split.at(nt))
                split.skip(nt)
                for k in range(2 * ns):
                    hc, (c0, cn) = k // ns, spans[k % ns]
                    pe.wait_ge(s_taken, taken.at(k - 1))
                    product(pp[k % 2][:, 0:cn],
                            lambda a, c: w16[:, a, W_1 + c * HID + hc * P:W_1 + c * HID + (hc + 1) * P],
                            lambda b, c: hT[b][:, c, c0:c0 + cn], KC).then_inc(s_pp, 1)
                taken.skip(2 * ns)
                pe.wait_ge(s_elo, e * NWP + NWP)
                pe.wait_ge(s_split, split.at(2 * ns))
                split.skip(2 * ns)
                for t in range(nt):
                    pe.wait_ge(s_taken, taken.at(max(t - 1, 0)))
                    product(pp[t % 2][:, :], lambda a, c: hid[a][:, c, t * P:(t + 1) * P],
                            lambda b, c: w16[:, b, W_2 + c * D:W_2 + (c + 1) * D], HID // P).then_inc(s_pp, 1)
                taken.skip(nt)
                pe.wait_ge(s_taken, taken.at(0))
                for r in counts:
                    r.settle()

            neg = Tally(pe, "pe_neg", 0)
            counts.append(neg)
            with nc.tensor.Fori(0, NE) as e:
                nb_e = nc.tensor.value_load(nblocks[0:1, bass.ds(e, 1)], min_val=1, max_val=NB)
                for nb in range(1, NB + 1):
                    with nc.tensor.If(nb_e == nb):
                        expert_pe(e, nb)

        @block.vector
        def _(dve):
            chain = [0]

            def link(ins):
                chain[0] += 1
                ins.then_inc(s_dch, 1)
                dve.wait_ge(s_dch, chain[0])

            dve.sem_inc(s_atlo, 2)
            dve.sem_inc(s_aggf, 2)
            dve.sem_inc(s_rc, 1)
            link(nc.vector.memset(span[:, :, :], FAR))
            dve.wait_ge(s_edges, 32)
            link(nc.vector.tensor_copy(edge[:, :, :], edge_i[:, :, :]))
            by_group = edge[:, 1, :].rearrange("p (g i) -> p g i", g=NG)
            nc.vector.tensor_reduce(span[0:TT, 0, :], by_group, AX.X, ALU.max)
            link(nc.vector.tensor_reduce(span[0:TT, 1, :], by_group, AX.X, ALU.min, negate=True))
            dve.sem_inc(s_span, 1)
            for t in range(NT):
                dve.wait_ge(s_x[t], 16)
                nc.vector.bn_stats(st6[0:TT, t, :], xn[:, t, :]).then_inc(s_st, 1)
            for t in range(NT):
                dve.wait_ge(s_st, t + 1)
                last = nc.vector.bn_aggr(mv[0:TT, t, :], st6[0:TT, t, :])
            link(last)
            nc.vector.tensor_scalar(mv[0:TT, :, 1], mv[0:TT, :, 1], EPS, None, ALU.add).then_inc(s_mv, 1)
            dve.wait_ge(s_span_all, 2)
            dve.wait_ge(s_const, 5)
            hi_all = span_all[0:1, 0, :].unsqueeze(1).broadcast_to([1, NT, NG])
            lo_all = span_all[0:1, 1, :].unsqueeze(1).broadcast_to([1, NT, NG])
            nc.vector.tensor_tensor(meet_f[:, 0], hi_all, tile0[:, :, :], ALU.is_ge)
            link(nc.vector.tensor_tensor(meet_f[:, 1], lo_all, tile0[:, :, :], ALU.add))
            link(nc.vector.tensor_scalar(meet_f[:, 1], meet_f[:, 1], float(-(TT - 1)), None, ALU.is_ge))
            link(nc.vector.tensor_tensor(meet_f[:, 0], meet_f[:, 0], meet_f[:, 1], ALU.mult))
            g_next = g1[0:1, :].unsqueeze(1).broadcast_to([1, NT, NG])
            link(nc.vector.scalar_tensor_tensor(meet_f[:, 1], g_next, float(-(NG + 1)), meet_f[:, 0],
                                                ALU.add, ALU.mult))
            nc.vector.tensor_reduce(edge_to[:, 0, :], meet_f[:, 1], AX.X, ALU.min)
            link(nc.vector.tensor_tensor(meet_f[:, 0], meet_f[:, 0], g_next, ALU.mult))
            link(nc.vector.tensor_reduce(edge_to[:, 1, :], meet_f[:, 0], AX.X, ALU.max))
            link(nc.vector.tensor_scalar(edge_to[:, 0, :], edge_to[:, 0, :], float(NG), None, ALU.add))
            nc.vector.tensor_copy(meets[:, :, :], edge_to[:, :, :]).then_inc(s_meets, 1)
            dve.wait_ge(s_rstd, 1)
            for t in range(NT):
                nc.vector.tensor_scalar(xn[:, t, :], xn[:, t, :], mv[0:TT, t, 0:1], rstd[0:TT, t:t + 1],
                                        ALU.subtract, ALU.mult).then_inc(s_xn, 1)
            for t in range(NT):
                dve.wait_ge(s_xthi, t + 1)
                cols = slice(t * TT, (t + 1) * TT)
                nc.vector.tensor_tensor(xnT_lo[:, :, cols],
                                        banks[6 + t % 2][:, 0:KC * TT].rearrange("p (c n) -> p c n", c=KC),
                                        xnT_hi[:, :, cols], ALU.subtract).then_inc(s_xtlo, 1)
            dve.wait_ge(s_meets, 1)
            for v in range(2):
                dve.sem_inc(s_ohused[v], 1)
            filled = dve.alloc_register("dve_filled")
            dve.reg_mov(filled, 1)

            def one_hots(t):
                first = nc.vector.value_load(meets[0:1, 0, bass.ds(t, 1)], min_val=0, max_val=2 * NG)
                end = nc.vector.value_load(meets[0:1, 1, bass.ds(t, 1)], min_val=0, max_val=NG)
                with nc.vector.Fori(0, NG // GS) as gs:
                    with nc.vector.If((gs * GS + GS > first) & (gs * GS < end)):
                        for gi in range(GS):
                            g = gs * GS + gi
                            with nc.vector.If((g >= first) & (g < end)):
                                fill = nc.vector.snap(filled)
                                for v in range(2):
                                    dve.wait_ge(s_ohused[v], fill)
                                    for i in range(GH):
                                        c = g * G + (v * GH + i)
                                        nc.vector.tensor_scalar(oh_src[:, v, i, :], iota[:, :],
                                                                edge[:, 0, bass.ds(c, 1)], None, ALU.is_equal)
                                        last = nc.vector.tensor_scalar(oh_dst[:, v, i, :],
                                                                       iota[:, bass.ds(t * TT, TT)],
                                                                       edge[:, 1, bass.ds(c, 1)], None, ALU.is_equal)
                                    last.then_inc(s_oh[v], 1)
                                dve.reg_add(filled, filled, 1)

            def low_counts(t, u):
                for k, (s0, sn) in enumerate(AT_COLS):
                    dve.wait_ge(s_athi, t * 3 + (k + 1))
                    nc.vector.tensor_tensor(at_lo[:, s0:s0 + sn, bass.ds(t * TT, TT)],
                                            b_at[(3 * u + k) % 2][0:TT, 0:sn * TT].rearrange("p (s n) -> p s n", s=sn),
                                            at_hi[:, s0:s0 + sn, bass.ds(t * TT, TT)],
                                            ALU.subtract).then_inc(s_atlo, 1)

            one_hots(0)
            with nc.vector.Fori(0, NT // 2 - 1) as tt:
                for u in range(2):
                    one_hots(tt * 2 + u + 1)
                    low_counts(tt * 2 + u, u)
            one_hots(NT - 1)
            low_counts(NT - 2, 0)
            low_counts(NT - 1, 1)
            with nc.vector.Fori(0, NB) as b:
                dve.wait_ge(s_cnt, b + 1)
                nc.vector.tensor_scalar(rc[:, 0, :], banks[2][:, 0:BW], 1.0, None, ALU.max).then_inc(s_rc0, 1)
                dve.wait_ge(s_rc0, b + 1)
                nc.vector.reciprocal(rc[:, 1, :], rc[:, 0, :]).then_inc(s_rc, 1)
                dve.wait_ge(s_rc, b + 2)
                for c in range(KC):
                    dve.wait_ge(s_sum, b * KC + (c + 1))
                    dve.wait_ge(s_agglo, b * KC + (c + 1))
                    nc.vector.tensor_tensor(agg_f[:, c % 2, :], banks[c % 2][:, 0:BW], rc[:, 1, :],
                                            ALU.mult).then_inc(s_aggf, 1)
            with nc.vector.Fori(0, NB) as b:
                for c in range(KC):
                    dve.wait_ge(s_hT, b * KC + (c + 3))
                    nc.vector.bn_stats(bn6[:, c, bass.ds(b, 1), :], h_gnn[:, c, bass.ds(b * BW, BW)]).then_inc(s_bn6, 1)
            dve.wait_ge(s_bn6, NB * KC)
            for c in range(KC):
                last = nc.vector.bn_aggr(bnmv[:, c, :], bn6[:, c, :, :].rearrange("p b s -> p (b s)"))
            link(last)
            nc.vector.tensor_scalar(bnmv[:, :, 1], bnmv[:, :, 1], EPS, None, ALU.add).then_inc(s_bn, 1)
            dve.wait_ge(s_bnr, 1)
            link(nc.vector.tensor_tensor(scale[:, :], bnr[:, :], par[:, 1, :], ALU.mult))
            link(nc.vector.tensor_tensor(shift[:, :], bnmv[:, :, 0], scale[:, :], ALU.mult))
            nc.vector.tensor_tensor(shift[:, :], par[:, 2, :], shift[:, :], ALU.subtract).then_inc(s_scale, 1)
            for t in range(NT):
                dve.wait_ge(s_back, t + 1)
                dve.wait_ge(s_xagain[t % 2], 16 * (t // 2 + 1))
                if t == 0:
                    dve.wait_ge(s_wlo, 2)
                nc.vector.tensor_tensor(x2[:, t, :], banks[2 + t % 2][0:TT, :], x_again[:, t % 2, :],
                                        ALU.add).then_inc(s_x2, 1)

            def row_stats(src_rows, stage):
                for t in range(NT):
                    last = nc.vector.bn_stats(rst6[:, t, :], src_rows(t)).then_inc(s_rst, 1)
                for t in range(NT):
                    dve.wait_ge(s_rst, stage * NT + t + 1)
                    last = nc.vector.bn_aggr(rmv[:, t, :], rst6[:, t, :])
                link(last)
                nc.vector.tensor_scalar(rmv[:, :, 1], rmv[:, :, 1], EPS, None, ALU.add).then_inc(s_rmv, 1)
                dve.wait_ge(s_rr, stage + 1)

            dve.wait_ge(s_x2, NT)
            row_stats(lambda t: x2[:, t, :], 0)
            for t in range(NT):
                nc.vector.tensor_scalar(rows[:, t, 0:D], x2[:, t, :], rmv[:, t, 0:1], rrstd[:, t:t + 1],
                                        ALU.subtract, ALU.mult).then_inc(s_xf, 1)
            dve.wait_ge(s_xf, NT)
            row_stats(lambda t: rows[:, t, 0:D], 1)
            for t in range(NT):
                nc.vector.tensor_scalar(rows[:, t, D:2 * D], rows[:, t, 0:D], rmv[:, t, 0:1], rrstd[:, t:t + 1],
                                        ALU.subtract, ALU.mult).then_inc(s_rn, 1)
            dve.wait_ge(s_gate, 32)
            for t in range(NT):
                for e in range(NE):
                    i = t * NE + e
                    if i >= 2:
                        dve.wait_ge(s_logit, i - 1)
                    nc.vector.tensor_tensor_reduce(out=prod[:, i % 2, :], in0=rows[:, t, 0:D],
                                                   in1=gate[:, e * D:(e + 1) * D], scale=1.0,
                                                   scalar=gate_bias[:, e:e + 1], op0=ALU.mult, op1=ALU.add,
                                                   accum_out=logit[:, e, t:t + 1]).then_inc(s_logit, 1)
            dve.wait_ge(s_logit, NE * NT)
            for e in range(NE):
                mine = logit[:, e, :].unsqueeze(1)
                link(nc.vector.memset(beats[:, e, :, e:e + 1], 0.0))
                if e > 0:
                    nc.vector.tensor_tensor(beats[:, e, :, 0:e].rearrange("p t j -> p j t"), logit[:, 0:e, :],
                                            mine.broadcast_to([TT, e, NT]), ALU.is_ge)
                if e < NE - 1:
                    last = nc.vector.tensor_tensor(beats[:, e, :, e + 1:NE].rearrange("p t j -> p j t"),
                                                   logit[:, e + 1:NE, :],
                                                   mine.broadcast_to([TT, NE - 1 - e, NT]), ALU.is_gt)
            link(nc.vector.memset(tile_base[:, :, :, 0:1], 0.0))
            link(nc.vector.tensor_reduce(rank[:, :, :], beats[:, :, :, :], AX.X, ALU.add))
            for k in range(2):
                last = nc.vector.tensor_scalar(member[:, k, :, :], rank[:, :, :], float(k), None, ALU.is_equal)
            link(last)
            nc.vector.tensor_copy(member_h[:, :, :, :], member[:, :, :, :]).then_inc(s_member, 1)
            for k in range(2):
                last = nc.vector.tensor_tensor(masked[:, k, :, :], member[:, k, :, :], logit[:, :, :], ALU.mult)
            link(last)
            for k in range(2):
                last = nc.vector.tensor_reduce(best[:, k, :], masked[:, k, :, :].rearrange("p e t -> p t e"),
                                               AX.X, ALU.add)
            link(last)
            nc.vector.tensor_tensor(gap[:, 0, :], best[:, 1, :], best[:, 0, :], ALU.subtract).then_inc(s_gap, 1)
            dve.wait_ge(s_ex, 1)
            link(nc.vector.tensor_scalar(gap[:, 2, :], gap[:, 1, :], 1.0, None, ALU.add))
            link(nc.vector.reciprocal(gap[:, 3, :], gap[:, 2, :]))
            nc.vector.tensor_copy(probs[:, :, 0], gap[:, 3, :])
            nc.vector.tensor_tensor(probs[:, :, 1], gap[:, 1, :], gap[:, 3, :], ALU.mult)
            dve.wait_ge(s_pref, 1)
            dve.wait_ge(s_tot, 1)
            nc.vector.tensor_copy(before[:, :, :, :].rearrange("p k e t -> p (k e t)"),
                                  banks[0][0:TT, 0:2 * NE * NT])
            link(nc.vector.tensor_copy(tile_sum[:, :, :, :].rearrange("p k e t -> p (k e t)"),
                                       banks[1][:, 0:2 * NE * NT]))
            for t in range(NT):
                link(nc.vector.tensor_tensor(tile_base[:, :, :, t + 1], tile_base[:, :, :, t], tile_sum[:, :, :, t],
                                             ALU.add))
            link(nc.vector.tensor_tensor(before[:, :, :, :], before[:, :, :, :], tile_base[0:TT, :, :, 0:NT], ALU.add))
            link(nc.vector.tensor_tensor(before[:, 1, :, :], before[:, 1, :, :],
                                         tile_base[0:TT, 0, :, NT:NT + 1].broadcast_to([TT, NE, NT]), ALU.add))
            dve.wait_ge(s_tri, 5)
            for k in range(2):
                last = nc.vector.tensor_tensor(before[:, k, :, :], before[:, k, :, :], list0[:, :, :], ALU.add)
            link(last)
            link(nc.vector.tensor_tensor(masked[:, :, :, :], before[:, :, :, :], member[:, :, :, :], ALU.mult))
            for k in range(2):
                last = nc.vector.tensor_reduce(slot_f[:, k, :], masked[:, k, :, :].rearrange("p e t -> p t e"),
                                               AX.X, ALU.add)
            link(last)
            nc.vector.tensor_copy(slots[:, :, :].rearrange("p t k -> p k t"), slot_f[:, :, :]).then_inc(s_slots, 1)
            link(nc.vector.tensor_tensor(total[:, :], tile_base[:, 0, :, NT], tile_base[:, 1, :, NT], ALU.add))
            link(nc.vector.tensor_tensor(pad_f[:, :, :], pad_iota[:, :, :],
                                         total[:, :].unsqueeze(2).broadcast_to([P, NE, 2]), ALU.add))
            nc.vector.tensor_copy(pad_row[:, :, :], pad_f[:, :, :]).then_inc(s_pads, 1)
            link(nc.vector.memset(blocks_f[:, 0, :], 1.0))
            for b in range(1, NB):
                link(nc.vector.tensor_scalar(blocks_f[:, 1, :], total[0:1, :], float(b * LB), None, ALU.is_gt))
                link(nc.vector.tensor_tensor(blocks_f[:, 0, :], blocks_f[:, 0, :], blocks_f[:, 1, :], ALU.add))
            nc.vector.tensor_copy(nblocks[:, :], blocks_f[:, 0, :]).then_inc(s_nblocks, 1)
            dve.wait_ge(s_rr, 2)
            nc.vector.tensor_tensor(own[:, 0, :], tile_base[0:NE, 0, :, NT], ident[0:NE, 0:NE], ALU.mult)
            link(nc.vector.tensor_tensor(own[:, 1, :], total[0:NE, :], ident[0:NE, 0:NE], ALU.mult))
            link(nc.vector.tensor_reduce(bound[:, :], own[:, :, :], AX.X, ALU.add))
            nc.vector.tensor_scalar(in_grp[:, 0, :], pos[:, :], bound[:, 0:1], None, ALU.is_lt)
            link(nc.vector.tensor_scalar(in_grp[:, 1, :], pos[:, :], bound[:, 1:2], None, ALU.is_lt))
            link(nc.vector.tensor_tensor(in_grp[:, 1, :], in_grp[:, 1, :], in_grp[:, 0, :], ALU.subtract))
            link(nc.vector.tensor_scalar(marks[:, 0, :, :], in_grp[:, :, :], BIG, None, ALU.mult))
            nc.vector.tensor_scalar(marks[:, 1, :, :], in_grp[:, :, :], BIG, -BIG, ALU.mult,
                                    ALU.add).then_inc(s_marks, 1)

            dve.wait_ge(s_nblocks, 1)
            dve.wait_ge(s_routed, 1)
            dve.wait_ge(s_epar, 16)
            dve.wait_ge(s_econst, 9)
            dve.sem_inc(s_split, 2)
            dve.sem_inc(s_mx, 2)
            dve.sem_inc(s_on, 2)
            dve.sem_inc(s_fin, 1)
            filled = Tally(dve, "dve_ppfilled", 0)
            taken = Tally(dve, "dve_taken", 2)
            qkp = Tally(dve, "dve_qkp", 2)
            steps = Tally(dve, "dve_steps", 0)
            scored = Tally(dve, "dve_scored", 0)
            maxed = Tally(dve, "dve_maxed", 2)
            scored_t = Tally(dve, "dve_scored_t", 1)
            summed = Tally(dve, "dve_summed", 4)
            on = Tally(dve, "dve_on", 2)
            biased = Tally(dve, "dve_biased", 0)
            heads = Tally(dve, "dve_heads", 0)
            counts = [heads, filled, taken, qkp, steps, scored, maxed, scored_t, summed, on, biased]

            def step(ins):
                ins.then_inc(s_ech, 1)
                steps.skip(1)
                dve.wait_ge(s_ech, steps.at(0))

            def split_columns(t, count_at):
                dve.wait_ge(s_taken, taken.at(count_at))
                cols = slice(t * P, (t + 1) * P)
                src_t = t32[:, t % 2, :].rearrange("p (c n) -> p c n", c=KC)
                step(nc.vector.tensor_copy(hT[0][:, :, cols], src_t))
                nc.vector.tensor_tensor(hT[1][:, :, cols], src_t, hT[0][:, :, cols],
                                        ALU.subtract).then_inc(s_split, 1)

            def expert_dve(e, nb):
                spans, nt = spans_of(nb), 2 * nb
                ns = len(spans)
                nx = ns * nt
                for t in range(nt):
                    split_columns(t, t + 1)
                taken.skip(2 * nt)
                filled.skip(2 * nt)
                splits.skip(nt)
                for r in counts:
                    r.settle()
                with nc.vector.Fori(0, H // 2) as j:
                    nc.vector.tensor_copy(ep_pair[:, :].unsqueeze(2), ep[:, BQ:L2W].rearrange(
                        "p (a j) -> p a j", a=3)[:, :, bass.ds(j, 1)]).then_inc(s_pair, 1)
                    for k in range(2 * ns):
                        s, side = k // 2, k % 2
                        c0, cn = spans[s]
                        cols = slice(c0, c0 + cn)
                        scaled, copied = taken.at(k + 1), qkp.at(k - 1)
                        dve.wait_ge(s_taken, scaled)
                        dve.wait_ge(s_qkp, copied)
                        high, low = halves[:, k % 2, 0, 0:cn], halves[:, k % 2, 1, 0:cn]
                        step(nc.vector.tensor_copy(high, t32[:, k % 2, 0:cn]))
                        nc.vector.tensor_tensor(low, t32[:, k % 2, 0:cn], high, ALU.subtract).then_inc(s_split, 1)
                        if k == 0:
                            dve.wait_ge(s_sT, scored_t.at(0))
                        if side == 0:
                            nc.vector.tensor_copy(q_hi[0:HD, 1, cols], high[HD:P])
                            nc.vector.tensor_copy(q_both[0:HD, 1, cols], high[HD:P])
                            dve.wait_ge(s_split, splits.at(k + 1))
                            nc.vector.tensor_copy(q_both[HD:P, 0, cols], low[0:HD])
                            last = nc.vector.tensor_copy(q_both[HD:P, 1, cols], low[HD:P])
                        else:
                            nc.vector.tensor_copy(k_hi[0:HD, 1, cols], high[HD:P])
                            nc.vector.tensor_copy(k_both[HD:P, 0, cols], high[0:HD])
                            nc.vector.tensor_copy(k_both[HD:P, 1, cols], high[HD:P])
                            dve.wait_ge(s_split, splits.at(k + 1))
                            last = nc.vector.tensor_copy(k_both[0:HD, 1, cols], low[HD:P])
                        last.then_inc(s_qkd, 1)
                    taken.skip(2 * ns + 2 * ns)
                    filled.skip(2 * ns + 2 * ns)
                    qkp.skip(2 * ns)
                    splits.skip(2 * ns)

                    def maximum(hd, i):
                        t, s = i // ns, i % ns
                        x = hd * nx + i
                        dve.wait_ge(s_s, scored.at(x + 1))
                        nc.vector.tensor_reduce(mx[:, hd, t, s:s + 1], sbk[x % 2][:, 0:spans[s][1]], AX.X,
                                                ALU.max).then_inc(s_mx, 1)

                    def maxima(hd):
                        dve.wait_ge(s_mx, maxed.at((hd + 1) * nx))
                        nc.vector.tensor_reduce(neg_max[:, hd, 0:nt], mx[:, hd, 0:nt, 0:ns], AX.X, ALU.max,
                                                negate=True).then_inc(s_neg, 1)

                    def divide(hd, s):
                        c0, cn = spans[s]
                        x = hd * ns + s
                        cols, part = slice(c0, c0 + cn), slice(hd * HD, (hd + 1) * HD)
                        bv = ep_pair[part, 2:3]
                        o_hi, o_lo = (m[part, bass.ds(j, 1), cols] for m in oT)
                        rows_o = o_tmp[part, x % 2:x % 2 + 1, 0:cn]
                        dve.wait_ge(s_pv, summed.at(hd * nx + (s + 1) * nt))
                        step(nc.vector.reciprocal(rcp[:, x % 2, 0:cn], pvb[x % 2][HD:P, 0:cn]))
                        nc.vector.tensor_tensor(o_tmp[part, x % 2, 0:cn], pvb[x % 2][0:HD, 0:cn],
                                                rcp[:, x % 2, 0:cn], ALU.mult).then_inc(s_on, 1)
                        dve.wait_ge(s_on, on.at(x + 1))
                        step(nc.vector.tensor_scalar(o_hi, rows_o, bv, None, ALU.add))
                        nc.vector.scalar_tensor_tensor(o_lo, rows_o, bv, o_hi, ALU.add,
                                                       ALU.subtract).then_inc(s_oT, 1)

                    for i in range(nx):
                        maximum(0, i)
                    maxima(0)
                    for i in range(nx):
                        maximum(1, i)
                        if (i + 1) % nt == 0:
                            divide(0, i // nt)
                    maxima(1)
                    for s in range(ns):
                        divide(1, s)
                    dve.wait_ge(s_oT, heads.at(2 * ns))
                    heads.skip(2 * ns)
                    scored.skip(2 * nx)
                    maxed.skip(2 * nx)
                    scored_t.skip(2 * nx)
                    summed.skip(2 * nx)
                    on.skip(2 * ns)
                    for r in counts:
                        r.settle()
                for t in range(nt):
                    dve.wait_ge(s_xb, biased.at(t + 1))
                    dve.wait_ge(s_pp, filled.at(t + 1))
                    nc.vector.tensor_tensor(v_rows[:, t, :], pp[t % 2][:, :], v_rows[:, t, :],
                                            ALU.add).then_inc(s_taken, 1)
                    if t > 0:
                        dve.wait_ge(s_taken, taken.at(t))
                        nc.vector.bn_stats(l2st[:, t - 1, :], v_rows[:, t - 1, :])
                dve.wait_ge(s_taken, taken.at(nt))
                step(nc.vector.bn_stats(l2st[:, nt - 1, :], v_rows[:, nt - 1, :]))
                dve.sem_inc(s_idle, 1)
                biased.skip(nt)
                taken.skip(nt)
                filled.skip(nt)
                for t in range(nt):
                    last = nc.vector.bn_aggr(l2mv[:, t, :], l2st[:, t, :])
                step(last)
                nc.vector.tensor_scalar(l2mv[:, 0:nt, 1], l2mv[:, 0:nt, 1], EPS, None, ALU.add).then_inc(s_l2v, 1)
                dve.wait_ge(s_l2r, e + 1)
                for t in range(nt):
                    if t >= 2:
                        dve.wait_ge(s_pp, filled.at(t - 1))
                    nc.vector.tensor_scalar(n2[:, t % 2, :], v_rows[:, t, :], l2mv[:, t, 0:1], l2r[:, t:t + 1],
                                            ALU.subtract, ALU.mult).then_inc(s_n2, 1)
                    if t >= 1:
                        split_columns(t - 1, t)
                split_columns(nt - 1, nt)
                taken.skip(nt)
                filled.skip(nt)
                for k in range(2 * ns):
                    hc, (c0, cn) = k // ns, spans[k % ns]
                    dve.wait_ge(s_taken, taken.at(k + 1))
                    step(nc.vector.tensor_copy(hid[0][:, hc, c0:c0 + cn], t32[:, k % 2, 0:cn]))
                    nc.vector.tensor_tensor(hid[1][:, hc, c0:c0 + cn], t32[:, k % 2, 0:cn],
                                            hid[0][:, hc, c0:c0 + cn], ALU.subtract).then_inc(s_split, 1)
                taken.skip(2 * ns)
                filled.skip(2 * ns)
                for t in range(nt):
                    dve.wait_ge(s_xb, biased.at(t + 1))
                    dve.wait_ge(s_pp, filled.at(t + 1))
                    last = nc.vector.tensor_tensor(v_rows[:, t, :], pp[t % 2][:, :], v_rows[:, t, :],
                                                   ALU.add).then_inc(s_taken, 1)
                biased.skip(nt)
                taken.skip(nt)
                filled.skip(nt)
                dve.wait_ge(s_taken, taken.at(0))
                dve.sem_inc(s_fin, 1)
                splits.skip(nt + 2 * ns)
                for r in counts:
                    r.settle()

            splits = Tally(dve, "dve_splits", 2)
            counts.append(splits)
            with nc.vector.Fori(0, NE) as e:
                nb_e = nc.vector.value_load(nblocks[0:1, bass.ds(e, 1)], min_val=1, max_val=NB)
                step(nc.vector.tensor_copy(ep[:, :].unsqueeze(1), epar[:, bass.ds(e, 1), :]))
                nc.vector.tensor_scalar(ep[:, BQ:BK], ep[:, BQ:BK], HD ** -0.5, None, ALU.mult).then_inc(s_ep, 1)
                steps.settle()
                for nb in range(1, NB + 1):
                    with nc.vector.If(nb_e == nb):
                        expert_dve(e, nb)

            for t in range(NT):
                dve.wait_ge(s_xy[t % 2], 16 * (t // 2 + 1))
                dve.wait_ge(s_g[t % 2], 32 * (t // 2 + 1))
                if t >= 2:
                    dve.wait_ge(s_yout[t % 2], 16 * (t // 2))
                y = n2[0:TT, t % 2, :]
                step(nc.vector.scalar_tensor_tensor(y, probs_t[0:TT, 2 * (t % 2), :], probs[:, t, 0:1],
                                                    t32[0:TT, t % 2, :], ALU.mult, ALU.add))
                nc.vector.scalar_tensor_tensor(y, probs_t[0:TT, 2 * (t % 2) + 1, :], probs[:, t, 1:2], y,
                                               ALU.mult, ALU.add).then_inc(s_y, 1)


_INS = ['x', 'src', 'dst', 'gnn_w', 'gnn_par', 'gate_w', 'gate_b', 'ew', 'epar', 'erow']
_OUTS = [((N, D), 'float32')]


def kernel(**inputs):
    import numpy as _np
    import concourse.bacc as _bacc
    from concourse import mybir as _mybir
    from concourse.bass_utils import run_bass_kernel_spmd as _run

    def chunked(v):
        return v.reshape(-1, P).T

    def by_chunk(w):
        w = w.transpose(0, 2, 1)
        return w.reshape(NE, -1, P, w.shape[2]).transpose(0, 2, 1, 3).reshape(NE, P, -1)

    a = {k: _np.asarray(v) for k, v in inputs.items()}
    lay = {
        'x': a['x'],
        'src': a['src'].reshape(NCH, TT).T,
        'dst': a['dst'].reshape(NCH, TT).T,
        'gnn_w': _np.concatenate([a[k].T.reshape(KC, P, D).transpose(1, 0, 2).reshape(P, KC * D)
                                  for k in ('L0_gnn_W_l', 'L0_gnn_W_r')], 1),
        'gnn_par': _np.stack([chunked(a[k]) for k in ('L0_gnn_b_l', 'L0_gnn_gamma', 'L0_gnn_beta')], 1),
        'gate_w': a['L0_ffn_gate_w'],
        'gate_b': a['L0_ffn_gate_b'].reshape(1, NE),
        'ew': _np.concatenate([by_chunk(a['L0_ffn_' + k]) for k in ('in_proj_w', 'out_proj_w', 'mlp_w1', 'mlp_w2')], 2),
        'epar': _np.concatenate([a['L0_ffn_' + k].reshape(NE, -1, P).transpose(2, 0, 1) for k in (
            'ln1_w', 'ln1_b', 'in_proj_b', 'ln2_w', 'ln2_b', 'mlp_b1')], 2),
        'erow': _np.stack([a['L0_ffn_out_proj_b'], a['L0_ffn_mlp_b2']], 1),
    }
    nc = _bacc.Bacc("TRN2", target_bir_lowering=False, num_devices=1)
    arrays, args = {}, []
    for name in _INS:
        v = _np.ascontiguousarray(lay[name])
        arrays[f"in_{name}_dram"] = v
        args.append(nc.dram_tensor(f"in_{name}_dram", v.shape, _mybir.dt.from_np(v.dtype), kind="ExternalInput").ap())
    for i, (shape, dtype) in enumerate(_OUTS):
        dt = _mybir.dt.from_np(_np.dtype(dtype))
        args.append(nc.dram_tensor(f"out_{i}_dram", shape, dt, kind="ExternalOutput").ap())
    program(nc, *args)
    r = _run(nc, [arrays], core_ids=[0])
    return r.results[0]["out_0_dram"]
```

```python
from contextlib import ExitStack

import concourse.bass as bass
from concourse import mybir

F32 = mybir.dt.float32
F16 = mybir.dt.float16
I32 = mybir.dt.int32
ALU = mybir.AluOpType
ACT = mybir.ActivationFunctionType
AX = mybir.AxisListType

N = 1250
D = 512
P = 128
TT = 125
NT = N // TT
NB = 5
BW = N // NB
KC = D // P
E_EDGES = 20000
NCH = E_EDGES // TT
G = 8
NG = NCH // G
GS = 5
GH = G // 2
EPS = 1e-5
NE = 4
LB = 256
LW = NB * LB
DS = D + 2
BIG = 32768.0
LIST = 1536
H = 8
HD = D // H
HID = 256
NTL = LW // P
W_QKV = 0
W_OUT = KC * 3 * D
W_1 = W_OUT + KC * D
W_2 = W_1 + KC * HID
WCOLS = W_2 + HID // P * D
WP = 1024
WB = 5
NWP = WCOLS // WP
QKV_P, OUT_P, W1_P = (W_OUT - W_QKV) // WP, W_1 // WP, W_2 // WP
L1W, L1B, BQ, BK, BV, L2W, L2B, B1 = 0, 4, 8, 12, 16, 20, 24, 28
NPAR = 30
MARK = HD
SHIFT = 96
NPB = 4
FAR = -30000.0


class Tally:

    def __init__(self, engine, name, start=0):
        self.engine = engine
        self.reg = engine.alloc_register(name)
        engine.reg_mov(self.reg, start)
        self.off = 0

    def at(self, k):
        return self.engine.snap(self.reg) + (self.off + k)

    def skip(self, n):
        self.off += n

    def settle(self):
        if self.off:
            self.engine.reg_add(self.reg, self.reg, self.off)
        self.off = 0


def spans_of(nb):
    return [(c0, min(512, nb * LB - c0)) for c0 in range(0, nb * LB, 512)]


def scores_beside(nx, i):
    first = nx // 6 if nx > 4 else nx // 4
    return [k for k in (2 * (i - first), 2 * (i - first) + 1) if 0 <= k < nx]


def row_beside(nx):
    return min(nx - 1, nx // 6 + nx // 2 + 3)


def settle(self):
        if self.off:
            self.engine.reg_add(self.reg, self.reg, self.off)
        self.off = 0


def settle(tallies):
    for t in tallies:
        t.settle()


def program(nc, x, src, dst, gnn_w, gnn_par, gate_w, gate_b, ew, epar_d, erow, out):
    stack = ExitStack()
    with stack:
        def sem(name):
            return stack.enter_context(nc.semaphore(name))

        def sb(name, shape, dt, where=None):
            return (where or stack).enter_context(nc.sbuf_tensor(name, shape, dt))

        def dram(name, shape, dt):
            return nc.dram_tensor(name, shape, dt, kind="Internal").ap()

        marks_dram = dram("marks_dram", (NE, 2, 2, LW), F16)
        es = dram("es", (NE * LIST, D), F32)
        x2_dram = dram("x2_dram", (N, D), F32)
        lists = dram("lists", (NE * LIST, DS), F32)

        ident = sb("ident", [P, P], F32)
        nblocks = sb("nblocks", [1, NE], I32)
        slots = sb("slots", [TT, NT, 2], I32)
        probs = sb("probs", [TT, NT, 2], F32)
        x2_mem = sb("x2_mem", [P, NTL * DS], F32)
        x2 = x2_mem[0:TT, 0:NT * D].rearrange("p (t d) -> p t d", t=NT)
        w_raw = x2_mem[:, 0:2 * KC * D]
        banks = [stack.enter_context(nc.psum_tensor(f"bank{i}", [P, 512], F32)) for i in range(8)]

        gnn = ExitStack()
        big = sb("big", [P, NT * D], F32, gnn)
        xn = big[0:TT, :].rearrange("p (t d) -> p t d", t=NT)
        h_gnn = big[:, 0:KC * N].rearrange("p (c n) -> p c n", c=KC)
        xn_hi = sb("xn_hi", [TT, NT, D], F16, gnn)
        xn_lo = sb("xn_lo", [TT, NT, D], F16, gnn)
        xnT_hi = sb("xnT_hi", [P, KC, N], F16, gnn)
        xnT_lo = sb("xnT_lo", [P, KC, N], F16, gnn)
        at_hi = sb("at_hi", [TT, NT, N], F16, gnn)
        at_lo = sb("at_lo", [TT, NT, N], F16, gnn)
        onehot = sb("onehot", [P, 2 * KC * N], F16, gnn)
        oh_src = onehot[0:TT, :].rearrange("p (v g n) -> p v g n", v=2, g=GH)
        agg = onehot[:, :].rearrange("p (h c n) -> p h c n", h=2, c=KC)
        oh_dst = sb("oh_dst", [TT, 2, GH, TT], F16, gnn)
        iota = sb("iota", [TT, N], F16, gnn)
        edge_i = sb("edge_i", [TT, 2, NCH], I32, gnn)
        edge = sb("edge", [TT, 2, NCH], F32, gnn)
        a_row = sb("a_row", [TT, 2, N], F32, gnn)
        a_turn = sb("a_turn", [TT, 2, 4 * TT], F32, gnn)
        w_hi = sb("w_hi", [P, 2, KC, D], F16, gnn)
        w_lo = sb("w_lo", [P, 2, KC, D], F16, gnn)
        par = sb("par", [P, 3, KC], F32, gnn)
        span = sb("span", [P, 2, NG], F32, gnn)
        span_all = sb("span_all", [P, 2, NG], F32, gnn)
        tile0 = sb("tile0", [1, NT, NG], F32, gnn)
        meet_f = sb("meet_f", [1, 2, NT, NG], F32, gnn)
        meets = sb("meets", [1, 2, NT], I32, gnn)
        edge_to = sb("edge_to", [1, 2, NT], F32, gnn)
        g1 = sb("g1", [1, NG], F32, gnn)
        ones_h = sb("ones_h", [TT, P], F16, gnn)
        zrow = sb("zrow", [1, 640], F16, gnn)
        st6 = sb("st6", [P, NT, 6], F32, gnn)
        mv = sb("mv", [P, NT, 2], F32, gnn)
        half = sb("half", [P, NT], F32, gnn)
        rstd = sb("rstd", [P, NT], F32, gnn)
        bn6 = sb("bn6", [P, KC, NB, 6], F32, gnn)
        bnmv = sb("bnmv", [P, KC, 2], F32, gnn)
        bnr = sb("bnr", [P, KC], F32, gnn)
        scale = sb("scale", [P, KC], F32, gnn)
        shift = sb("shift", [P, KC], F32, gnn)
        rc = sb("rc", [P, 2, BW], F32, gnn)
        agg_f = sb("agg_f", [P, 2, BW], F32, gnn)
        x_again = sb("x_again", [TT, 2, D], F32, gnn)
        gnn.close()

        w_stage = sb("w_stage", [P, WB, WP], F32)
        w16 = sb("w16", [P, 2, WCOLS], F16)
        ident_h = sb("ident_h", [P, P], F16)
        q_hi = sb("q_hi", [P, 2, LW], F16)
        k_hi = sb("k_hi", [P, 2, LW], F16)
        v_head = sb("v_head", [P, 2, NTL, P], F32)
        zero_row = sb("zero_row", [P, D], F32)
        l2half = sb("l2half", [P, NTL], F32)
        route = ExitStack()
        rows = sb("rows", [TT, NT, DS], F32, route)
        gate = sb("gate", [TT, NE * D], F32, route)
        gate_bias = sb("gate_bias", [TT, NE], F32, route)
        prod = sb("prod", [TT, 2, D], F32, route)
        rst6 = sb("rst6", [TT, NT, 6], F32, route)
        rmv = sb("rmv", [TT, NT, 2], F32, route)
        rrstd = sb("rrstd", [TT, NT], F32, route)
        minus_half = sb("minus_half", [TT, NT], F32, route)
        logit = sb("logit", [TT, NE, NT], F32, route)
        beats = sb("beats", [TT, NE, NT, NE], F32, route)
        rank = sb("rank", [TT, NE, NT], F32, route)
        member = sb("member", [TT, 2, NE, NT], F32, route)
        member_h = sb("member_h", [TT, 2, NE, NT], F16, route)
        masked = sb("masked", [TT, 2, NE, NT], F32, route)
        best = sb("best", [TT, 2, NT], F32, route)
        gap = sb("gap", [TT, 4, NT], F32, route)
        tri = sb("tri", [TT, TT], F16, route)
        ones_r = sb("ones_r", [TT, P], F16, route)
        before = sb("before", [TT, 2, NE, NT], F32, route)
        tile_sum = sb("tile_sum", [P, 2, NE, NT], F32, route)
        tile_base = sb("tile_base", [P, 2, NE, NT + 1], F32, route)
        list0 = sb("list0", [TT, NE, NT], F32, route)
        slot_f = sb("slot_f", [TT, 2, NT], F32, route)
        total = sb("total", [P, NE], F32, route)
        pad_f = sb("pad_f", [P, NE, 2], F32, route)
        pad_row = sb("pad_row", [P, NE, 2], I32, route)
        pad_iota = sb("pad_iota", [P, NE, 2], F32, route)
        zeros = sb("zeros", [P, DS], F32, route)
        blocks_f = sb("blocks_f", [1, 2, NE], F32, route)
        pos = sb("pos", [NE, LW], F32, route)
        own = sb("own", [NE, 2, NE], F32, route)
        bound = sb("bound", [NE, 2], F32, route)
        in_grp = sb("in_grp", [NE, 2, LW], F32, route)
        marks = sb("marks", [NE, 2, 2, LW], F16, route)
        route.close()

        epar = sb("epar", [P, NE, NPAR], F32)
        ep = sb("ep", [P, NPAR], F32)
        ep_pair = sb("ep_pair", [P, 3], F32)
        hT = [sb(f"hT{i}", [P, KC, LW], F16) for i in range(2)]
        q_both = sb("q_both", [P, 2, LW], F16)
        k_both = sb("k_both", [P, 2, LW], F16)
        hid = [q_both, k_both]
        v_stat = x2_mem[:, :].rearrange("p (t d) -> p t d", t=NTL)
        v_rows = v_stat[:, :, 0:D]
        probs_t = sb("probs_t", [P, NPB, 512], F32)
        oT = [sb(f"oT{i}", [P, H // 2, LW], F16) for i in range(2)]
        n2 = sb("n2", [P, 2, D], F32)
        t32 = sb("t32", [P, 2, 512], F32)
        halves = sb("halves", [P, 2, 2, LW], F16)
        row_par = sb("row_par", [P, 2, D], F32)
        den = sb("den", [P, LW], F32)
        o_pair = sb("o_pair", [P, LW], F32)
        mx = sb("mx", [P, 2, NTL, 3], F32)
        neg_max = sb("neg_max", [P, 2, NTL], F16)
        l2st = sb("l2st", [P, NTL, 6], F32)
        l2mv = sb("l2mv", [P, NTL, 2], F32)
        l2r = sb("l2r", [P, NTL], F32)
        pp, sbk, stb, pvb = banks[0:2], banks[2:4], banks[4:6], banks[6:8]

        s_x = [sem(f"s_xin{t}") for t in range(NT)]
        s_edges = sem("s_edges")
        s_gw = sem("s_gw")
        s_par = sem("s_par")
        s_id = sem("s_id")
        s_const = sem("s_const")
        s_mv = sem("s_mv")
        s_rstd = sem("s_rstd")
        s_xn = sem("s_xn")
        s_xhi = sem("s_xhi")
        s_xlo = sem("s_xlo")
        s_whi = sem("s_whi")
        s_wlo = sem("s_wlo")
        s_xt = sem("s_xt")
        s_xthi = sem("s_xthi")
        s_xtlo = sem("s_xtlo")
        s_span = sem("s_span")
        s_span_all = sem("s_span_all")
        s_meets = sem("s_meets")
        s_dch = sem("s_dch")
        s_oh = [sem(f"s_oh{v}") for v in range(2)]
        s_ohused = [sem(f"s_ohused{v}") for v in range(2)]
        s_arow = sem("s_arow")
        s_acopy = sem("s_acopy")
        s_at = sem("s_at")
        s_athi = sem("s_athi")
        s_atlo = sem("s_atlo")
        s_cnt = sem("s_cnt")
        s_rc = sem("s_rc")
        s_sum = sem("s_sum")
        s_aggf = sem("s_aggf")
        s_agghi = sem("s_agghi")
        s_agglo = sem("s_agglo")
        s_rc0 = sem("s_rc0")
        s_st = sem("s_st")
        s_bn6 = sem("s_bn6")
        s_h = sem("s_h")
        s_hT = sem("s_hT")
        s_bn = sem("s_bn")
        s_bnr = sem("s_bnr")
        s_scale = sem("s_scale")
        s_relu = sem("s_relu")
        s_back = sem("s_back")
        s_xagain = [sem(f"s_xagain{i}") for i in range(2)]
        s_x2 = sem("s_x2")
        s_x2out = sem("s_x2out")
        s_pch = sem("s_pch")
        s_routed = sem("s_routed")
        s_epar = sem("s_epar")
        s_ep = sem("s_ep")
        s_pair = sem("s_pair")
        s_idle = sem("s_idle")
        s_ech = sem("s_ech")
        s_wst = [sem(f"s_wst{i}") for i in range(WB)]
        s_ehi = sem("s_ehi")
        s_elo = sem("s_elo")
        s_mk = sem("s_mk")
        s_rp = sem("s_rp")
        s_nr = [sem(f"s_nr{b}") for b in range(NB)]
        s_xr = sem("s_xr")
        s_es = [sem(f"s_es{b}") for b in range(NB)]
        s_esz = sem("s_esz")
        s_stored = sem("s_stored")
        s_econst = sem("s_econst")
        s_pp = sem("s_pp")
        s_taken = sem("s_taken")
        s_split = sem("s_split")
        s_qkd = sem("s_qkd")
        s_qkb = sem("s_qkb")
        s_vh = sem("s_vh")
        s_s = sem("s_s")
        s_mx = sem("s_mx")
        s_neg = sem("s_neg")
        s_sT = sem("s_sT")
        s_exp = sem("s_exp")
        s_pv = sem("s_pv")
        s_on = sem("s_on")
        s_oT = sem("s_oT")
        s_xb = sem("s_xb")
        s_l2v = sem("s_l2v")
        s_l2r = sem("s_l2r")
        s_n1 = sem("s_n1")
        s_n2 = sem("s_n2")
        s_fin = sem("s_fin")
        s_g = [sem(f"s_g{i}") for i in range(2)]
        s_xy = [sem(f"s_xy{i}") for i in range(2)]
        s_y = sem("s_y")
        s_yout = [sem(f"s_yout{i}") for i in range(2)]
        s_gate = sem("s_gate")
        s_rmv = sem("s_rmv")
        s_rr = sem("s_rr")
        s_xf = sem("s_xf")
        s_rn = sem("s_rn")
        s_rst = sem("s_rst")
        s_tri = sem("s_tri")
        s_gap = sem("s_gap")
        s_ex = sem("s_ex")
        s_member = sem("s_member")
        s_pref = sem("s_pref")
        s_tot = sem("s_tot")
        s_slots = sem("s_slots")
        s_pads = sem("s_pads")
        s_marks = sem("s_marks")
        s_marksout = sem("s_marksout")
        s_scat = sem("s_scat")
        s_nblocks = sem("s_nblocks")
        s_zero = sem("s_zero")
        s_rpch = sem("s_rpch")
        s_logit = sem("s_logit")

        w_r = w_raw.rearrange("p (m c n) -> p m c n", m=2, c=KC)
        x_t = x.rearrange("(t p) d -> p t d", p=TT)
        x2d_t = x2_dram.rearrange("(t p) d -> p t d", p=TT)
        b_at = [banks[6], banks[7]]
        ab = [banks[0:3], banks[3:6]]
        A_COLS = [(0, 512), (512, 512), (1024, N - 1024)]
        AT_COLS = [(0, 4), (4, 4), (8, 2)]

        block = stack.enter_context(nc.Block())

        @block.sync
        def _(sp):
            def load_piece(e, p):
                if isinstance(e, int):
                    if p >= WB:
                        sp.wait_ge(s_elo, p - WB + 1)
                    rows_of_e = ew[e:e + 1, :, :]
                else:
                    rows_of_e = ew[bass.ds(nc.s_assert_within(e, 0, NE - 1), 1), :, :]
                    sp.wait_ge(s_elo, e * NWP + (p - WB + 1))
                sp.dma_start(w_stage[:, p % WB, :], rows_of_e[:, :, p * WP:(p + 1) * WP].rearrange(
                    "a p n -> (a p) n")).then_inc(s_wst[p % WB], 16)

            sp.dma_start(edge_i[:, 0, :], src).then_inc(s_edges, 16)
            sp.dma_start(edge_i[:, 1, :], dst).then_inc(s_edges, 16)
            for t in range(NT):
                sp.dma_start(xn[:, t, :], x_t[:, t, :]).then_inc(s_x[t], 16)
            sp.dma_start(w_raw, gnn_w).then_inc(s_gw, 16)
            sp.dma_start(par[:, :, :], gnn_par).then_inc(s_par, 16)
            for t in range(NT):
                if t >= 2:
                    sp.wait_ge(s_x2, t - 1)
                sp.dma_start(x_again[:, t % 2, :], x_t[:, t, :]).then_inc(s_xagain[t % 2], 16)
            for t in range(NT):
                sp.wait_ge(s_x2, t + 1)
                sp.dma_start(x2d_t[:, t, :], x2[:, t, :]).then_inc(s_x2out, 16)
            sp.dma_start(gate[:, :], gate_w.partition_broadcast(TT)).then_inc(s_gate, 16)
            sp.dma_start(gate_bias[:, :], gate_b.partition_broadcast(TT)).then_inc(s_gate, 16)
            for p in range(QKV_P):
                load_piece(0, p)
            sp.wait_ge(s_marks, 1)
            sp.dma_start(marks_dram, marks[:, :, :, :]).then_inc(s_marksout, 16)
            sp.wait_ge(s_x2out, 16 * NT)
            sp.wait_ge(s_marksout, 16)
            sp.wait_ge(s_scat, 16 * (2 * NT + 2 * NE))
            sp.sem_inc(s_routed, 1)

            taken = Tally(sp, "sp_taken", 2)
            stored = [Tally(sp, f"sp_stored{b}", 16) for b in range(NB)]
            for b in range(NB):
                sp.sem_inc(s_es[b], 16)
            sp.dma_start(epar[:, :, :], epar_d).then_inc(s_epar, 16)
            sp.wait_ge(s_nblocks, 1)
            sp.wait_ge(s_econst, 9)

            def expert_sp(e, nb):
                for b in range(nb):
                    list_rows = lists[bass.ds(e * LIST + b * LB, LB), :].rearrange("(t p) d -> p t d", p=P)
                    sp.wait_ge(s_es[b], stored[b].at(0))
                    sp.sem_inc(s_idle, 1)
                    sp.dma_start(v_stat[:, 2 * b:2 * b + 2, :],
                                 list_rows).then_inc(s_nr[b], 16)
                for side, m in enumerate((q_hi, k_hi)):
                    for hd in range(2):
                        sp.dma_start(m[MARK:MARK + 2, hd, :], marks_dram[bass.ds(e, 1), side, :, :].rearrange(
                            "a r n -> (a r) n")).then_inc(s_mk, 16)
                sp.dma_start(row_par[:, :, :], erow[bass.ds(e, 1), :, :].partition_broadcast(P)).then_inc(s_rp, 16)
                for p in range(QKV_P, NWP):
                    load_piece(e, p)
                with sp.If(e < NE - 1):
                    for p in range(WB):
                        load_piece(e + 1, p)
                sp.dma_start(es[bass.ds(e * LIST + nb * LB, LIST - nb * LB), :].rearrange("(i p) d -> p i d", p=P),
                             zero_row[:, :].unsqueeze(1).broadcast_to([P, (LIST - nb * LB) // P, D])
                             ).then_inc(s_esz, 16)
                list_rows = lists[bass.ds(e * LIST, nb * LB), 0:D].rearrange("(t p) d -> p t d", p=P)
                sp.wait_ge(s_vh, e * H + H)
                sp.sem_inc(s_idle, 1)
                sp.dma_start(v_rows[:, 0:2 * nb, :], list_rows).then_inc(s_xr, 16)
                with sp.If(e < NE - 1):
                    for p in range(WB, QKV_P):
                        load_piece(e + 1, p)
                nt, ns = 2 * nb, len(spans_of(nb))
                taken.skip(4 * nt + 2 * H * ns + 2 * ns)
                for b in range(nb):
                    es_rows = es[bass.ds(e * LIST + b * LB, LB), :].rearrange("(t p) d -> p t d", p=P)
                    sp.wait_ge(s_taken, taken.at(2 * b + 2))
                    sp.sem_inc(s_idle, 1)
                    sp.dma_start(es_rows, v_rows[:, 2 * b:2 * b + 2, :]).then_inc(s_es[b], 16)
                    stored[b].skip(16)
                taken.skip(nt)
                for r in [taken] + stored:
                    r.settle()

            with sp.Fori(0, NE) as e:
                sp.wait_ge(s_fin, e + 1)
                nb_e = sp.value_load(nblocks[0:1, bass.ds(e, 1)], min_val=1, max_val=NB)
                for nb in range(1, NB + 1):
                    with sp.If(nb_e == nb):
                        expert_sp(e, nb)
            for b in range(NB):
                sp.wait_ge(s_es[b], stored[b].at(0))
                sp.sem_inc(s_idle, 1)
            sp.wait_ge(s_esz, 16 * NE)
            sp.sem_inc(s_stored, 1)

            def x2_again(t):
                sp.dma_start(t32[0:TT, t % 2, :], x2d_t[:, t, :]).then_inc(s_xy[t % 2], 16)

            x2_again(0)
            x2_again(1)
            for t in range(NT):
                sp.wait_ge(s_y, t + 1)
                sp.dma_start(out.rearrange("(t p) d -> p t d", p=TT)[:, t, :], n2[0:TT, t % 2, :]
                             ).then_inc(s_yout[t % 2], 16)
                if t + 2 < NT:
                    x2_again(t + 2)
            for i in range(2):
                sp.wait_ge(s_yout[i], 16 * (NT // 2))

        @block.gpsimd
        def _(pool):
            def low_weights(e, p):
                cols = slice(p * WP, (p + 1) * WP)
                pool.wait_ge(s_ehi, e * NWP + (p + 1))
                nc.gpsimd.tensor_tensor(w16[:, 1, cols], w_stage[:, p % WB, :], w16[:, 0, cols],
                                        ALU.subtract).then_inc(s_elo, 1)

            nc.gpsimd.memset(ident[:, :], 0.0).then_inc(s_pch, 1)
            nc.gpsimd.memset(half[:, :], -0.5).then_inc(s_pch, 1)
            nc.gpsimd.memset(ones_h[:, :], 1.0).then_inc(s_const, 1)
            nc.gpsimd.memset(zrow[:, :], 0.0).then_inc(s_const, 1)
            nc.gpsimd.iota(iota[:, :], pattern=[[1, N]], base=0, channel_multiplier=0,
                           allow_small_or_imprecise_dtypes=True).then_inc(s_const, 1)
            nc.gpsimd.iota(tile0[:, :, :], pattern=[[TT, NT], [0, NG]], base=0, channel_multiplier=0,
                           allow_small_or_imprecise_dtypes=True).then_inc(s_const, 1)
            nc.gpsimd.iota(g1[:, :], pattern=[[1, NG]], base=1, channel_multiplier=0,
                           allow_small_or_imprecise_dtypes=True).then_inc(s_const, 1)
            pool.wait_ge(s_pch, 2)
            nc.gpsimd.affine_select(out=ident[:, :], in_=ident[:, :], compare_op=ALU.not_equal, fill=1.0,
                                    base=0, pattern=[[-1, P]], channel_multiplier=1).then_inc(s_id, 1)
            pool.wait_ge(s_span, 1)
            for k in range(2):
                nc.gpsimd.partition_all_reduce(span_all[:, k, :], span[:, k, :], P,
                                               bass.bass_isa.ReduceOp.max).then_inc(s_span_all, 1)
            pool.wait_ge(s_mv, 1)
            nc.gpsimd.tensor_tensor(rstd[0:TT, :], mv[0:TT, :, 1], half[0:TT, :], ALU.pow).then_inc(s_rstd, 1)
            for t in range(NT):
                pool.wait_ge(s_xhi, t + 1)
                nc.gpsimd.tensor_tensor(xn_lo[:, t, :], xn[:, t, :], xn_hi[:, t, :], ALU.subtract).then_inc(s_xlo, 1)
            for m in range(2):
                pool.wait_ge(s_whi, m + 1)
                nc.gpsimd.tensor_tensor(w_lo[:, m, :, :], w_r[:, m, :, :], w_hi[:, m, :, :],
                                        ALU.subtract).then_inc(s_wlo, 1)
            pool.sem_inc(s_atlo, 2)
            with nc.gpsimd.Fori(0, NT // 2) as tt:
                for u in range(2):
                    t = tt * 2 + u
                    for k, (s0, sn) in enumerate(AT_COLS):
                        pool.wait_ge(s_athi, t * 3 + (k + 3))
                        pool.sem_inc(s_idle, 1)
                        nc.gpsimd.tensor_tensor(at_lo[:, s0:s0 + sn, bass.ds(t * TT, TT)],
                                                a_turn[:, (3 * u + k) % 2, 0:sn * TT].rearrange(
                                                    "p (s n) -> p s n", s=sn),
                                                at_hi[:, s0:s0 + sn, bass.ds(t * TT, TT)],
                                                ALU.subtract).then_inc(s_atlo, 1)
            pool.sem_inc(s_agglo, 2)
            with nc.gpsimd.Fori(0, NB) as b:
                for c in range(KC):
                    pool.wait_ge(s_agghi, b * KC + (c + 1))
                    nc.gpsimd.tensor_tensor(agg[:, 1, c, bass.ds(b * BW, BW)], agg_f[:, c % 2, :],
                                            agg[:, 0, c, bass.ds(b * BW, BW)], ALU.subtract).then_inc(s_agglo, 1)
            pool.wait_ge(s_bn, 1)
            nc.gpsimd.tensor_tensor(bnr[:, :], bnmv[:, :, 1], half[:, 0:KC], ALU.pow).then_inc(s_bnr, 1)

            pool.wait_ge(s_x2, NT)
            nc.gpsimd.memset(minus_half[:, :], -0.5).then_inc(s_rpch, 1)
            nc.gpsimd.memset(tri[:, :], 1.0).then_inc(s_rpch, 1)
            nc.gpsimd.memset(ones_r[:, :], 1.0).then_inc(s_tri, 1)
            nc.gpsimd.iota(list0[:, :, :], pattern=[[LIST, NE], [0, NT]], base=0, channel_multiplier=0,
                           allow_small_or_imprecise_dtypes=True).then_inc(s_tri, 1)
            nc.gpsimd.iota(pad_iota[:, :, :], pattern=[[LIST, NE], [P, 2]], base=0, channel_multiplier=1,
                           allow_small_or_imprecise_dtypes=True).then_inc(s_tri, 1)
            nc.gpsimd.iota(pos[:, :], pattern=[[1, LW]], base=0, channel_multiplier=0,
                           allow_small_or_imprecise_dtypes=True).then_inc(s_tri, 1)
            pool.wait_ge(s_rpch, 2)
            nc.gpsimd.affine_select(out=tri[:, :], in_=tri[:, :], compare_op=ALU.is_gt, fill=0.0,
                                    base=0, pattern=[[1, TT]], channel_multiplier=-1).then_inc(s_tri, 1)
            pool.wait_ge(s_rmv, 1)
            nc.gpsimd.tensor_tensor(rrstd[:, :], rmv[:, :, 1], minus_half[:, :], ALU.pow).then_inc(s_rr, 1)
            nc.gpsimd.memset(zeros[:, :], 0.0).then_inc(s_zero, 1)
            pool.wait_ge(s_rmv, 2)
            nc.gpsimd.tensor_tensor(rows[:, :, D + 1], rmv[:, :, 1], minus_half[:, :], ALU.pow).then_inc(s_rr, 1)
            for p in range(QKV_P):
                low_weights(0, p)
            nc.gpsimd.tensor_copy(ident_h[:, :], ident[:, :]).then_inc(s_econst, 1)
            nc.gpsimd.memset(q_hi[:, :, :], 0.0).then_inc(s_econst, 1)
            nc.gpsimd.memset(k_hi[:, :, :], 0.0).then_inc(s_econst, 1)
            nc.gpsimd.memset(v_head[:, :, :, :], 1.0).then_inc(s_econst, 1)
            nc.gpsimd.memset(l2half[:, :], -0.5).then_inc(s_econst, 1)
            nc.gpsimd.memset(zero_row[:, :], 0.0).then_inc(s_econst, 1)
            pool.wait_ge(s_econst, 6)
            nc.gpsimd.memset(k_hi[SHIFT:SHIFT + 1, :, :], 1.0).then_inc(s_econst, 3)
            pool.wait_ge(s_econst, 9)
            pool.wait_ge(s_slots, 1)
            pool.wait_ge(s_rn, 1)
            pool.wait_ge(s_rr, 2)
            for t in range(NT):
                for k in range(2):
                    nc.gpsimd.indirect_dma_start(
                        out=lists, out_offset=bass.IndirectOffsetOnAxis(ap=slots[:, t, k:k + 1], axis=0),
                        in_=rows[:, t, :], in_offset=None, bounds_check=NE * LIST - 1,
                        oob_is_err=False).then_inc(s_scat, 16)
            pool.wait_ge(s_zero, 1)
            pool.wait_ge(s_pads, 1)
            for e in range(NE):
                for i in range(2):
                    nc.gpsimd.indirect_dma_start(
                        out=lists, out_offset=bass.IndirectOffsetOnAxis(ap=pad_row[:, e, i:i + 1], axis=0),
                        in_=zeros[:, :], in_offset=None, bounds_check=NE * LIST - 1,
                        oob_is_err=False).then_inc(s_scat, 16)

            pool.wait_ge(s_routed, 1)
            taken = Tally(pool, "pool_taken", 2)
            summed = Tally(pool, "pool_summed", 4)
            normed = Tally(pool, "pool_normed", 0)

            def expert_pool(e, nb):
                spans, nt = spans_of(nb), 2 * nb
                ns = len(spans)
                taken.skip(2 * nt)
                pool.wait_ge(s_taken, taken.at(0))
                taken.settle()

                def copy_values(j, hd):
                    nc.gpsimd.tensor_copy(v_head[:, hd, 0:nt, hd * HD:(hd + 1) * HD],
                                          v_rows[:, 0:nt, bass.ds(j * P + hd * HD, HD)]).then_inc(s_vh, 1)

                def after_head():
                    summed.skip(ns * nt)
                    pool.wait_ge(s_pv, summed.at(0))
                    pool.sem_inc(s_idle, 1)

                for hd in range(2):
                    nc.gpsimd.tensor_copy(v_head[:, hd, 0:nt, hd * HD:(hd + 1) * HD], v_rows[:, 0:nt, hd * HD:(hd + 1) * HD]
                                          ).then_inc(s_vh, 1)
                for p in range(QKV_P, NWP):
                    low_weights(e, p)
                summed.settle()
                with nc.gpsimd.Fori(0, H // 2 - 1) as j:
                    after_head()
                    copy_values(j + 1, 0)
                    after_head()
                    copy_values(j + 1, 1)
                    summed.settle()
                summed.skip(2 * ns * nt)
                pool.wait_ge(s_xr, e * 16 + 16)
                pool.wait_ge(s_rp, e * 16 + 16)
                for t in range(nt):
                    nc.gpsimd.tensor_tensor(v_rows[:, t, :], v_rows[:, t, :], row_par[:, 0, :],
                                            ALU.add).then_inc(s_xb, 1)
                with nc.gpsimd.If(e < NE - 1):
                    for p in range(QKV_P // 2):
                        low_weights(e + 1, p)
                pool.wait_ge(s_l2v, e + 1)
                nc.gpsimd.tensor_tensor(l2r[:, 0:nt], l2mv[:, 0:nt, 1], l2half[:, 0:nt], ALU.pow).then_inc(s_l2r, 1)
                with nc.gpsimd.If(e < NE - 1):
                    for p in range(QKV_P // 2, QKV_P):
                        low_weights(e + 1, p)
                for t in range(nt):
                    pool.wait_ge(s_n2, normed.at(t + 1))
                    nc.gpsimd.tensor_tensor(v_rows[:, t, :], v_rows[:, t, :], row_par[:, 1, :],
                                            ALU.add).then_inc(s_xb, 1)
                normed.skip(nt)
                taken.skip(8 * ns * 2 + 3 * nt + 2 * ns)
                for r in (taken, normed, summed):
                    r.settle()

            with nc.gpsimd.Fori(0, NE) as e:
                nb_e = nc.gpsimd.value_load(nblocks[0:1, bass.ds(e, 1)], min_val=1, max_val=NB)
                for nb in range(1, NB + 1):
                    with nc.gpsimd.If(nb_e == nb):
                        expert_pool(e, nb)

            pool.wait_ge(s_stored, 1)
            for t in range(NT):
                if t >= 2:
                    pool.wait_ge(s_y, t - 1)
                for k in range(2):
                    nc.gpsimd.indirect_dma_start(
                        out=probs_t[0:TT, 2 * (t % 2) + k, :], out_offset=None, in_=es,
                        in_offset=bass.IndirectOffsetOnAxis(ap=slots[:, t, k:k + 1], axis=0),
                        bounds_check=NE * LIST - 1, oob_is_err=False).then_inc(s_g[t % 2], 16)

        @block.scalar
        def _(act):
            def high_weights(e, p):
                act.wait_ge(s_wst[p % WB], e * (16 * NWP // WB) + 16 * (p // WB + 1))
                nc.scalar.copy(w16[:, 0, p * WP:(p + 1) * WP], w_stage[:, p % WB, :]).then_inc(s_ehi, 1)

            act.sem_inc(s_acopy, 2)
            act.sem_inc(s_athi, 2)
            act.sem_inc(s_hT, 2)
            for t in range(NT):
                act.wait_ge(s_xn, t + 1)
                nc.scalar.copy(xn_hi[:, t, :], xn[:, t, :]).then_inc(s_xhi, 1)
            for t in range(NT):
                act.wait_ge(s_xt, t + 1)
                nc.scalar.copy(xnT_hi[:, :, t * TT:(t + 1) * TT],
                               banks[6 + t % 2][:, 0:KC * TT].rearrange("p (c n) -> p c n", c=KC)).then_inc(s_xthi, 1)
            act.wait_ge(s_gw, 16)
            for m in range(2):
                nc.scalar.copy(w_hi[:, m, :, :], w_r[:, m, :, :]).then_inc(s_whi, 1)

            def copy_rows(t, u):
                act.wait_ge(s_arow, t + 1)
                for k, (c0, cn) in enumerate(A_COLS):
                    last = nc.scalar.copy(a_row[:, u, c0:c0 + cn], ab[u][k][0:TT, 0:cn])
                last.then_inc(s_acopy, 1)

            def high_counts(t, u):
                for k, (s0, sn) in enumerate(AT_COLS):
                    r = (3 * u + k) % 2
                    transposed, split = t * 3 + (k + 1), t * 3 + (k + 1)
                    act.wait_ge(s_at, transposed)
                    act.wait_ge(s_atlo, split)
                    nc.scalar.copy(a_turn[:, r, 0:sn * TT], b_at[r][0:TT, 0:sn * TT])
                    nc.scalar.copy(at_hi[:, s0:s0 + sn, bass.ds(t * TT, TT)],
                                   b_at[r][0:TT, 0:sn * TT].rearrange("p (s n) -> p s n", s=sn)
                                   ).then_inc(s_athi, 1)

            copy_rows(0, 0)
            with nc.scalar.Fori(0, NT // 2 - 1) as tt:
                for u in range(2):
                    copy_rows(tt * 2 + u + 1, 1 - u)
                    high_counts(tt * 2 + u, u)
            copy_rows(NT - 1, 1)
            high_counts(NT - 2, 0)
            high_counts(NT - 1, 1)
            with nc.scalar.Fori(0, NB) as b:
                for c in range(KC):
                    act.wait_ge(s_aggf, b * KC + (c + 3))
                    nc.scalar.copy(agg[:, 0, c, bass.ds(b * BW, BW)], agg_f[:, c % 2, :]).then_inc(s_agghi, 1)
            act.wait_ge(s_par, 16)
            with nc.scalar.Fori(0, NB) as b:
                for c in range(KC):
                    act.wait_ge(s_h, b * KC + (c + 1))
                    nc.scalar.activation(h_gnn[:, c, bass.ds(b * BW, BW)], banks[c % 2][:, 0:BW], ACT.Identity,
                                         bias=par[:, 0, c:c + 1]).then_inc(s_hT, 1)
            act.wait_ge(s_scale, 1)
            for c in range(KC):
                nc.scalar.activation(h_gnn[:, c, :], h_gnn[:, c, :], ACT.Relu, bias=shift[:, c:c + 1],
                                     scale=scale[:, c:c + 1]).then_inc(s_relu, 1)

            for p in range(QKV_P):
                high_weights(0, p)
            act.wait_ge(s_gap, 1)
            nc.scalar.activation(gap[:, 1, :], gap[:, 0, :], ACT.Exp).then_inc(s_ex, 1)

            act.wait_ge(s_nblocks, 1)
            act.wait_ge(s_routed, 1)
            act.wait_ge(s_econst, 9)
            act.sem_inc(s_taken, 2)
            act.sem_inc(s_exp, 2)
            filled = Tally(act, "act_filled", 0)
            split = Tally(act, "act_split", 2)
            divided = Tally(act, "act_divided", 1)
            act.sem_inc(s_on, 2)
            scored = Tally(act, "act_scored", 1)
            summed = Tally(act, "act_summed", 4)

            def scaled_columns(nt, w0, b0):
                for t in range(nt):
                    act.wait_ge(s_pp, filled.at(t + 1))
                    act.wait_ge(s_split, split.at(t - 1))
                    for c in range(KC):
                        last = nc.scalar.activation(t32[:, t % 2, c * P:(c + 1) * P], pp[t % 2][:, c * P:(c + 1) * P],
                                                    ACT.Identity, bias=ep[:, b0 + c:b0 + c + 1],
                                                    scale=ep[:, w0 + c:w0 + c + 1])
                    last.then_inc(s_taken, 1)
                filled.skip(nt)
                split.skip(nt)

            def expert_act(e, nb):
                spans, nt = spans_of(nb), 2 * nb
                ns = len(spans)
                nx = ns * nt
                act.wait_ge(s_ep, e + 1)
                act.wait_ge(s_fin, e + 1)
                scaled_columns(nt, L1W, L1B)
                act.wait_ge(s_split, split.at(0))
                for t in range(nt):
                    act.wait_ge(s_pp, filled.at(t + 1))
                    nc.scalar.copy(v_rows[:, t, :], pp[t % 2][:, :]).then_inc(s_taken, 1)
                filled.skip(nt)
                for p in range(QKV_P, NWP):
                    high_weights(e, p)
                for r in (filled, split):
                    r.settle()

                def scaled_pair(pair, first):
                    act.wait_ge(s_pair, pair)
                    for k in range(2 * ns):
                        s, side = k // 2, k % 2
                        cn = spans[s][1]
                        act.wait_ge(s_pp, filled.at(k + 1))
                        act.wait_ge(s_split, split.at(k - 1))
                        nc.scalar.activation(t32[:, k % 2, 0:cn], pp[(first + k) % 2][:, 0:cn], ACT.Identity,
                                             bias=ep_pair[:, side:side + 1],
                                             scale=(HD ** -0.5, 1.0)[side]).then_inc(s_taken, 1)
                    filled.skip(2 * ns)
                    split.skip(2 * ns)

                def copy_maxima(hd):
                    for s, (c0, cn) in enumerate(spans):
                        act.wait_ge(s_pp, filled.at(s + 1))
                        nc.scalar.copy(q_hi[SHIFT:SHIFT + 1, hd, c0:c0 + cn],
                                       pp[(hd * ns + s) % 2][0:1, 0:cn]).then_inc(s_taken, 1)
                    filled.skip(ns)

                def copy_sums(hd, s):
                    (c0, cn), bank = spans[s], pvb[(hd * ns + s) % 2]
                    mine, other = slice(hd * HD, (hd + 1) * HD), slice((1 - hd) * HD, (2 - hd) * HD)
                    made, free = summed.at((s + 1) * nt), divided.at(0)
                    act.wait_ge(s_pv, made)
                    act.wait_ge(s_oT, free)
                    nc.scalar.copy(o_pair[mine, c0:c0 + cn], bank[mine, 0:cn])
                    nc.scalar.copy(den[mine, c0:c0 + cn], bank[other, 0:cn]).then_inc(s_on, 1)

                def exponentials(hd, beside):
                    for i in range(nx):
                        x = hd * nx + i
                        cn = spans[i // nt][1]
                        act.wait_ge(s_sT, scored.at(i + 1))
                        act.wait_ge(s_pv, summed.at(i - 3))
                        nc.scalar.activation(probs_t[:, x % NPB, 0:cn], stb[x % 2][:, 0:cn],
                                             ACT.Exp).then_inc(s_exp, 1)
                        if i % nt == 2 and i > nt:
                            copy_sums(hd, i // nt - 1)
                        if beside is not None and i == row_beside(nx):
                            copy_maxima(beside)
                    copy_sums(hd, ns - 1)
                    if hd == 1:
                        divided.skip(ns)
                    scored.skip(nx)
                    summed.skip(nx)

                scaled_pair(e * (H // 2) + 1, 0)
                copy_maxima(0)
                for r in (filled, split):
                    r.settle()
                with nc.scalar.Fori(0, H // 2 - 1) as j:
                    exponentials(0, None)
                    scaled_pair(e * (H // 2) + j + 2, ns)
                    copy_maxima(1)
                    exponentials(1, 0)
                    for r in (filled, split, scored, summed, divided):
                        r.settle()
                exponentials(0, None)
                copy_maxima(1)
                exponentials(1, None)
                act.wait_ge(s_sT, scored.at(0))
                act.sem_inc(s_idle, 1)
                with nc.scalar.If(e < NE - 1):
                    for p in range(QKV_P):
                        high_weights(e + 1, p)
                filled.skip(nt)
                scaled_columns(nt, L2W, L2B)
                for k in range(2 * ns):
                    hc, s = k // ns, k % ns
                    cn = spans[s][1]
                    act.wait_ge(s_pp, filled.at(k + 1))
                    act.wait_ge(s_split, split.at(k - 1))
                    nc.scalar.activation(t32[:, k % 2, 0:cn], pp[k % 2][:, 0:cn], ACT.Gelu,
                                         bias=ep[:, B1 + hc:B1 + hc + 1]).then_inc(s_taken, 1)
                filled.skip(2 * ns)
                split.skip(2 * ns)
                filled.skip(nt)
                for r in (filled, split, scored, summed, divided):
                    r.settle()

            with nc.scalar.Fori(0, NE) as e:
                nb_e = nc.scalar.value_load(nblocks[0:1, bass.ds(e, 1)], min_val=1, max_val=NB)
                for nb in range(1, NB + 1):
                    with nc.scalar.If(nb_e == nb):
                        expert_act(e, nb)

        @block.tensor
        def _(pe):
            pe.wait_ge(s_id, 1)
            for t in range(NT):
                pe.wait_ge(s_xn, t + 1)
                if t >= 2:
                    pe.wait_ge(s_xtlo, t - 1)
                for c in range(KC):
                    last = nc.tensor.transpose(banks[6 + t % 2][:, c * TT:(c + 1) * TT],
                                               xn[:, t, c * P:(c + 1) * P], ident[0:TT, 0:TT])
                last.then_inc(s_xt, 1)
            pe.wait_ge(s_const, 5)
            pe.wait_ge(s_meets, 1)
            filled = pe.alloc_register("pe_filled")
            pe.reg_mov(filled, 1)

            def count_rows(t, u):
                pe.wait_ge(s_acopy, t + 1)
                for k, (c0, cn) in enumerate(A_COLS):
                    nc.tensor.matmul(ab[u][k][0:TT, 0:cn], zrow[0:1, 0:TT], zrow[0:1, 0:cn], start=True, stop=True,
                                     skip_group_check=True)
                first = nc.tensor.value_load(meets[0:1, 0, bass.ds(t, 1)], min_val=0, max_val=2 * NG)
                end = nc.tensor.value_load(meets[0:1, 1, bass.ds(t, 1)], min_val=0, max_val=NG)
                with nc.tensor.Fori(0, NG // GS) as gs:
                    with nc.tensor.If((gs * GS + GS > first) & (gs * GS < end)):
                        for gi in range(GS):
                            g = gs * GS + gi
                            with nc.tensor.If((g >= first) & (g < end)):
                                fill = nc.tensor.snap(filled)
                                for v in range(2):
                                    pe.wait_ge(s_oh[v], fill)
                                    for i in range(GH):
                                        for k, (c0, cn) in enumerate(A_COLS):
                                            last = nc.tensor.matmul(ab[u][k][0:TT, 0:cn], oh_dst[:, v, i, :],
                                                                    oh_src[:, v, i, c0:c0 + cn], start=False,
                                                                    stop=True, skip_group_check=True)
                                    last.then_inc(s_ohused[v], 1)
                                pe.reg_add(filled, filled, 1)
                nc.tensor.matmul(ab[u][0][0:TT, 0:1], zrow[0:1, 0:TT], zrow[0:1, 0:1], start=False, stop=True,
                                 skip_group_check=True).then_inc(s_arow, 1)

            def turn_rows(t, u):
                pe.wait_ge(s_acopy, t + 3)
                for k, (s0, sn) in enumerate(AT_COLS):
                    pe.wait_ge(s_athi, t * 3 + (k + 1))
                    for s in range(sn):
                        last = nc.tensor.transpose(b_at[(3 * u + k) % 2][0:TT, s * TT:(s + 1) * TT],
                                                   a_row[:, u, (s0 + s) * TT:(s0 + s + 1) * TT], ident[0:TT, 0:TT])
                    last.then_inc(s_at, 1)

            pe.wait_ge(s_xtlo, NT)
            count_rows(0, 0)
            with nc.tensor.Fori(0, NT // 2 - 1) as tt:
                for u in range(2):
                    count_rows(tt * 2 + u + 1, 1 - u)
                    turn_rows(tt * 2 + u, u)
            count_rows(NT - 1, 1)
            turn_rows(NT - 2, 0)
            turn_rows(NT - 1, 1)

            pe.wait_ge(s_xlo, NT)
            pe.wait_ge(s_atlo, 3 * NT + 2)
            with nc.tensor.Fori(0, NB) as b:
                pe.wait_ge(s_rc, b + 1)
                for k, m in enumerate([at_hi, at_lo]):
                    for s in range(NT):
                        last = nc.tensor.matmul(banks[2][:, 0:BW], ones_h[:, :], m[:, s, bass.ds(b * BW, BW)],
                                                start=(k == 0 and s == 0), stop=(k == 1 and s == NT - 1))
                last.then_inc(s_cnt, 1)
                for c in range(KC):
                    pe.wait_ge(s_aggf, b * KC + (c + 1))
                    for k, (w, m) in enumerate([(xn_hi, at_hi), (xn_lo, at_hi), (xn_hi, at_lo)]):
                        for s in range(NT):
                            last = nc.tensor.matmul(banks[c % 2][:, 0:BW], w[:, s, c * P:(c + 1) * P],
                                                    m[:, s, bass.ds(b * BW, BW)],
                                                    start=(k == 0 and s == 0), stop=(k == 2 and s == NT - 1))
                    last.then_inc(s_sum, 1)
            pe.wait_ge(s_wlo, 2)
            pe.wait_ge(s_agglo, NB * KC + 2)
            with nc.tensor.Fori(0, NB) as b:
                for c in range(KC):
                    pe.wait_ge(s_hT, b * KC + (c + 1))
                    for m, (hi, lo) in enumerate([(agg[:, 0], agg[:, 1]), (xnT_hi, xnT_lo)]):
                        for k, (w, a) in enumerate([(w_hi, hi), (w_lo, hi), (w_hi, lo)]):
                            for j in range(KC):
                                last = nc.tensor.matmul(banks[c % 2][:, 0:BW], w[:, m, j, c * P:(c + 1) * P],
                                                        a[:, j, bass.ds(b * BW, BW)],
                                                        start=(m == 0 and k == 0 and j == 0),
                                                        stop=(m == 1 and k == 2 and j == KC - 1))
                    last.then_inc(s_h, 1)
            for t in range(NT):
                if t == 0:
                    pe.wait_ge(s_relu, KC)
                if t >= 2:
                    pe.wait_ge(s_x2, t - 1)
                for c in range(KC):
                    last = nc.tensor.transpose(banks[2 + t % 2][0:TT, c * P:(c + 1) * P],
                                               h_gnn[:, c, t * TT:(t + 1) * TT], ident[:, :])
                last.then_inc(s_back, 1)

            pe.wait_ge(s_member, 1)
            pe.wait_ge(s_tri, 5)
            members = member_h[:, :, :, :].rearrange("p k e t -> p (k e t)")
            nc.tensor.matmul(banks[0][0:TT, 0:2 * NE * NT], tri[:, :], members, start=True, stop=True).then_inc(s_pref, 1)
            nc.tensor.matmul(banks[1][:, 0:2 * NE * NT], ones_r[:, :], members, start=True, stop=True).then_inc(s_tot, 1)

            pe.wait_ge(s_nblocks, 1)
            pe.wait_ge(s_routed, 1)
            pe.wait_ge(s_econst, 9)
            pe.wait_ge(s_slots, 1)
            pe.sem_inc(s_sT, 1)
            pe.sem_inc(s_pv, 4)
            normed1 = Tally(pe, "pe_normed1", 0)
            taken = Tally(pe, "pe_taken", 2)
            split = Tally(pe, "pe_split", 2)
            maxed = Tally(pe, "pe_maxed", 2)
            exped = Tally(pe, "pe_exped", 2)
            on = Tally(pe, "pe_on", 2)
            oT_done = Tally(pe, "pe_oT", 1)
            qkd = Tally(pe, "pe_qkd", 0)
            qkb = Tally(pe, "pe_qkb", 0)
            normed = Tally(pe, "pe_normed", 0)
            counts = [normed1, taken, split, maxed, exped, on, oT_done, qkd, qkb, normed]
            PASSES = [(0, 0), (1, 0), (0, 1)]

            def product(bank, lhs, rhs, chunks):
                for n, (a, b) in enumerate(PASSES):
                    for c in range(chunks):
                        last = nc.tensor.matmul(bank, lhs(a, c), rhs(b, c), start=(n == 0 and c == 0),
                                                stop=(n == 2 and c == chunks - 1))
                return last

            def turn(rows_of, t):
                for c in range(KC):
                    last = nc.tensor.transpose(pp[t % 2][:, c * P:(c + 1) * P], rows_of[:, c * P:(c + 1) * P],
                                               ident[:, :])
                last.then_inc(s_pp, 1)

            def expert_pe(e, nb):
                spans, nt = spans_of(nb), 2 * nb
                ns = len(spans)
                nx = ns * nt
                for t in range(nt):
                    pe.wait_ge(s_taken, taken.at(t - 1))
                    pe.wait_ge(s_n1, normed1.at(t + 1))
                    turn(v_rows[:, t, :], t)
                taken.skip(nt)
                normed1.skip(nt)
                pe.wait_ge(s_elo, e * NWP + QKV_P)
                pe.wait_ge(s_split, split.at(nt))
                split.skip(nt)
                for t in range(nt):
                    pe.wait_ge(s_taken, taken.at(t - 1))
                    product(pp[t % 2][:, :], lambda a, c: hT[a][:, c, t * P:(t + 1) * P],
                            lambda b, c: w16[:, b, c * 3 * D + 2 * D:(c + 1) * 3 * D], KC).then_inc(s_pp, 1)
                taken.skip(nt)
                for r in counts:
                    r.settle()

                def project(j, first):
                    for k in range(2 * ns):
                        s, side = k // 2, k % 2
                        c0, cn = spans[s]
                        pe.wait_ge(s_taken, taken.at(k - 1))
                        product(pp[(first + k) % 2][:, 0:cn],
                                lambda a, c: w16[:, a, bass.ds(j * P + (c * 3 * D + side * D), P)],
                                lambda b, c: hT[b][:, c, c0:c0 + cn], KC).then_inc(s_pp, 1)
                        if k == 0 and first and ns == 1:
                            for i in range(nx):
                                scores(1, i)
                    taken.skip(2 * ns)
                    split.skip(2 * ns)

                def scores(hd, i):
                    t, (c0, cn) = i // ns, spans[i % ns]
                    if i == 0:
                        if hd == 0:
                            pe.wait_ge(s_qkd, qkd.at(2 * ns))
                            qkd.skip(2 * ns)
                        else:
                            pe.wait_ge(s_qkb, qkb.at(1))
                            qkb.skip(1)
                    pe.wait_ge(s_mx, maxed.at(i - 1))
                    nc.tensor.matmul(sbk[i % 2][:, 0:cn], q_hi[0:MARK + 2, hd, t * P:(t + 1) * P],
                                     k_hi[0:MARK + 2, hd, c0:c0 + cn], start=True, stop=True).then_inc(s_s, 1)
                    if i == nx - 1:
                        maxed.skip(nx)

                def maxima_row(hd):
                    pe.wait_ge(s_neg, neg.at(1))
                    neg.skip(1)
                    for s, (c0, cn) in enumerate(spans):
                        pe.wait_ge(s_taken, taken.at(s - 1))
                        for i in range(cn // P):
                            t = c0 // P + i
                            last = nc.tensor.matmul(pp[(hd * ns + s) % 2][0:1, i * P:(i + 1) * P],
                                                    neg_max[:, hd, t:t + 1], ident_h[:, :], start=True, stop=True)
                        last.then_inc(s_pp, 1)
                    taken.skip(ns)

                def scores_t(hd, i):
                    s, kt = i // nt, i % nt
                    c0, cn = spans[s]
                    pe.wait_ge(s_exp, exped.at(i - 1))
                    nc.tensor.matmul(stb[i % 2][:, 0:cn], k_hi[0:SHIFT + 1, hd, kt * P:(kt + 1) * P],
                                     q_hi[0:SHIFT + 1, hd, c0:c0 + cn], start=True, stop=False)
                    nc.tensor.matmul(stb[i % 2][:, 0:cn], k_both[:, hd, kt * P:(kt + 1) * P],
                                     q_both[:, hd, c0:c0 + cn], start=False, stop=True).then_inc(s_sT, 1)

                def sums(hd, i, copied):
                    s, kt = i // nt, i % nt
                    cn = spans[s][1]
                    divided, made = on.at(s - 1), exped.at(i + 1)
                    if i == 0:
                        pe.wait_ge(s_vh, copied)
                    if kt == 0:
                        pe.wait_ge(s_on, divided)
                    pe.wait_ge(s_exp, made)
                    nc.tensor.matmul(pvb[(hd * ns + s) % 2][:, 0:cn], v_head[:, hd, kt, :],
                                     probs_t[:, (hd * nx + i) % NPB, 0:cn], start=(kt == 0),
                                     stop=(kt == nt - 1)).then_inc(s_pv, 1)

                def attend(j, hd, beside):
                    copied = e * H + j * 2 + (hd + 1)
                    pe.wait_ge(s_taken, taken.at(0))
                    scores_t(hd, 0)
                    scores_t(hd, 1)
                    for i in range(nx):
                        sums(hd, i, copied)
                        if i + 2 < nx:
                            scores_t(hd, i + 2)
                        if beside is not None:
                            for k in scores_beside(nx, i):
                                scores(beside, k)
                            if beside == 0 and i == row_beside(nx):
                                maxima_row(beside)
                    exped.skip(nx)
                    on.skip(ns)

                project(0, 0)
                pe.wait_ge(s_mk, e * 64 + 64)
                for i in range(nx):
                    scores(0, i)
                maxima_row(0)
                for r in counts:
                    r.settle()
                with nc.tensor.Fori(0, H // 2 - 1) as j:
                    attend(j, 0, 1 if ns > 1 else None)
                    project(j + 1, ns)
                    maxima_row(1)
                    attend(j, 1, 0)
                    for r in counts:
                        r.settle()
                attend(H // 2 - 1, 0, 1)
                maxima_row(1)
                attend(H // 2 - 1, 1, None)
                oT_done.skip(H // 2 * ns)
                heads, emptied, split_up = oT_done.at(0), taken.at(0), e * NWP + OUT_P
                pe.wait_ge(s_oT, heads)
                pe.wait_ge(s_taken, emptied)
                pe.wait_ge(s_elo, split_up)
                for t in range(nt):
                    if t >= 2:
                        pe.wait_ge(s_taken, taken.at(t - 1))
                    product(pp[t % 2][:, :], lambda a, c: oT[a][:, c, t * P:(t + 1) * P],
                            lambda b, c: w16[:, b, W_OUT + c * D:W_OUT + (c + 1) * D], KC).then_inc(s_pp, 1)
                taken.skip(nt)
                for t in range(nt):
                    pe.wait_ge(s_taken, taken.at(max(t - 1, 0)))
                    pe.wait_ge(s_n2, normed.at(t + 1))
                    turn(n2[:, t % 2, :], t)
                taken.skip(nt)
                normed.skip(nt)
                pe.wait_ge(s_elo, e * NWP + W1_P)
                pe.wait_ge(s_split, split.at(nt))
                split.skip(nt)
                for k in range(2 * ns):
                    hc, (c0, cn) = k // ns, spans[k % ns]
                    pe.wait_ge(s_taken, taken.at(k - 1))
                    product(pp[k % 2][:, 0:cn],
                            lambda a, c: w16[:, a, W_1 + c * HID + hc * P:W_1 + c * HID + (hc + 1) * P],
                            lambda b, c: hT[b][:, c, c0:c0 + cn], KC).then_inc(s_pp, 1)
                taken.skip(2 * ns)
                pe.wait_ge(s_elo, e * NWP + NWP)
                pe.wait_ge(s_split, split.at(2 * ns))
                split.skip(2 * ns)
                for t in range(nt):
                    pe.wait_ge(s_taken, taken.at(max(t - 1, 0)))
                    product(pp[t % 2][:, :], lambda a, c: hid[a][:, c, t * P:(t + 1) * P],
                            lambda b, c: w16[:, b, W_2 + c * D:W_2 + (c + 1) * D], HID // P).then_inc(s_pp, 1)
                taken.skip(nt)
                pe.wait_ge(s_taken, taken.at(0))
                for r in counts:
                    r.settle()

            neg = Tally(pe, "pe_neg", 0)
            counts.append(neg)
            with nc.tensor.Fori(0, NE) as e:
                nb_e = nc.tensor.value_load(nblocks[0:1, bass.ds(e, 1)], min_val=1, max_val=NB)
                for nb in range(1, NB + 1):
                    with nc.tensor.If(nb_e == nb):
                        expert_pe(e, nb)

        @block.vector
        def _(dve):
            chain = [0]

            def link(ins):
                chain[0] += 1
                ins.then_inc(s_dch, 1)
                dve.wait_ge(s_dch, chain[0])

            dve.sem_inc(s_aggf, 2)
            dve.sem_inc(s_rc, 1)
            link(nc.vector.memset(span[:, :, :], FAR))
            dve.wait_ge(s_edges, 32)
            link(nc.vector.tensor_copy(edge[:, :, :], edge_i[:, :, :]))
            by_group = edge[:, 1, :].rearrange("p (g i) -> p g i", g=NG)
            nc.vector.tensor_reduce(span[0:TT, 0, :], by_group, AX.X, ALU.max)
            link(nc.vector.tensor_reduce(span[0:TT, 1, :], by_group, AX.X, ALU.min, negate=True))
            dve.sem_inc(s_span, 1)
            for t in range(NT):
                dve.wait_ge(s_x[t], 16)
                nc.vector.bn_stats(st6[0:TT, t, :], xn[:, t, :]).then_inc(s_st, 1)
            for t in range(NT):
                dve.wait_ge(s_st, t + 1)
                last = nc.vector.bn_aggr(mv[0:TT, t, :], st6[0:TT, t, :])
            link(last)
            nc.vector.tensor_scalar(mv[0:TT, :, 1], mv[0:TT, :, 1], EPS, None, ALU.add).then_inc(s_mv, 1)
            dve.wait_ge(s_span_all, 2)
            dve.wait_ge(s_const, 5)
            hi_all = span_all[0:1, 0, :].unsqueeze(1).broadcast_to([1, NT, NG])
            lo_all = span_all[0:1, 1, :].unsqueeze(1).broadcast_to([1, NT, NG])
            nc.vector.tensor_tensor(meet_f[:, 0], hi_all, tile0[:, :, :], ALU.is_ge)
            link(nc.vector.tensor_tensor(meet_f[:, 1], lo_all, tile0[:, :, :], ALU.add))
            link(nc.vector.tensor_scalar(meet_f[:, 1], meet_f[:, 1], float(-(TT - 1)), None, ALU.is_ge))
            link(nc.vector.tensor_tensor(meet_f[:, 0], meet_f[:, 0], meet_f[:, 1], ALU.mult))
            g_next = g1[0:1, :].unsqueeze(1).broadcast_to([1, NT, NG])
            link(nc.vector.scalar_tensor_tensor(meet_f[:, 1], g_next, float(-(NG + 1)), meet_f[:, 0],
                                                ALU.add, ALU.mult))
            nc.vector.tensor_reduce(edge_to[:, 0, :], meet_f[:, 1], AX.X, ALU.min)
            link(nc.vector.tensor_tensor(meet_f[:, 0], meet_f[:, 0], g_next, ALU.mult))
            link(nc.vector.tensor_reduce(edge_to[:, 1, :], meet_f[:, 0], AX.X, ALU.max))
            link(nc.vector.tensor_scalar(edge_to[:, 0, :], edge_to[:, 0, :], float(NG), None, ALU.add))
            nc.vector.tensor_copy(meets[:, :, :], edge_to[:, :, :]).then_inc(s_meets, 1)
            dve.wait_ge(s_rstd, 1)
            for t in range(NT):
                nc.vector.tensor_scalar(xn[:, t, :], xn[:, t, :], mv[0:TT, t, 0:1], rstd[0:TT, t:t + 1],
                                        ALU.subtract, ALU.mult).then_inc(s_xn, 1)
            for t in range(NT):
                dve.wait_ge(s_xthi, t + 1)
                cols = slice(t * TT, (t + 1) * TT)
                nc.vector.tensor_tensor(xnT_lo[:, :, cols],
                                        banks[6 + t % 2][:, 0:KC * TT].rearrange("p (c n) -> p c n", c=KC),
                                        xnT_hi[:, :, cols], ALU.subtract).then_inc(s_xtlo, 1)
            dve.wait_ge(s_meets, 1)
            for v in range(2):
                dve.sem_inc(s_ohused[v], 1)
            filled = dve.alloc_register("dve_filled")
            dve.reg_mov(filled, 1)

            def one_hots(t):
                first = nc.vector.value_load(meets[0:1, 0, bass.ds(t, 1)], min_val=0, max_val=2 * NG)
                end = nc.vector.value_load(meets[0:1, 1, bass.ds(t, 1)], min_val=0, max_val=NG)
                with nc.vector.Fori(0, NG // GS) as gs:
                    with nc.vector.If((gs * GS + GS > first) & (gs * GS < end)):
                        for gi in range(GS):
                            g = gs * GS + gi
                            with nc.vector.If((g >= first) & (g < end)):
                                fill = nc.vector.snap(filled)
                                for v in range(2):
                                    dve.wait_ge(s_ohused[v], fill)
                                    for i in range(GH):
                                        c = g * G + (v * GH + i)
                                        nc.vector.tensor_scalar(oh_src[:, v, i, :], iota[:, :],
                                                                edge[:, 0, bass.ds(c, 1)], None, ALU.is_equal)
                                        last = nc.vector.tensor_scalar(oh_dst[:, v, i, :],
                                                                       iota[:, bass.ds(t * TT, TT)],
                                                                       edge[:, 1, bass.ds(c, 1)], None, ALU.is_equal)
                                    last.then_inc(s_oh[v], 1)
                                dve.reg_add(filled, filled, 1)

            with nc.vector.Fori(0, NT) as t:
                one_hots(t)
            with nc.vector.Fori(0, NB) as b:
                dve.wait_ge(s_cnt, b + 1)
                nc.vector.tensor_scalar(rc[:, 0, :], banks[2][:, 0:BW], 1.0, None, ALU.max).then_inc(s_rc0, 1)
                dve.wait_ge(s_rc0, b + 1)
                nc.vector.reciprocal(rc[:, 1, :], rc[:, 0, :]).then_inc(s_rc, 1)
                dve.wait_ge(s_rc, b + 2)
                for c in range(KC):
                    dve.wait_ge(s_sum, b * KC + (c + 1))
                    dve.wait_ge(s_agglo, b * KC + (c + 1))
                    nc.vector.tensor_tensor(agg_f[:, c % 2, :], banks[c % 2][:, 0:BW], rc[:, 1, :],
                                            ALU.mult).then_inc(s_aggf, 1)
            with nc.vector.Fori(0, NB) as b:
                for c in range(KC):
                    dve.wait_ge(s_hT, b * KC + (c + 3))
                    nc.vector.bn_stats(bn6[:, c, bass.ds(b, 1), :], h_gnn[:, c, bass.ds(b * BW, BW)]).then_inc(s_bn6, 1)
            dve.wait_ge(s_bn6, NB * KC)
            for c in range(KC):
                last = nc.vector.bn_aggr(bnmv[:, c, :], bn6[:, c, :, :].rearrange("p b s -> p (b s)"))
            link(last)
            nc.vector.tensor_scalar(bnmv[:, :, 1], bnmv[:, :, 1], EPS, None, ALU.add).then_inc(s_bn, 1)
            dve.wait_ge(s_bnr, 1)
            link(nc.vector.tensor_tensor(scale[:, :], bnr[:, :], par[:, 1, :], ALU.mult))
            link(nc.vector.tensor_tensor(shift[:, :], bnmv[:, :, 0], scale[:, :], ALU.mult))
            nc.vector.tensor_tensor(shift[:, :], par[:, 2, :], shift[:, :], ALU.subtract).then_inc(s_scale, 1)
            for t in range(NT):
                dve.wait_ge(s_back, t + 1)
                dve.wait_ge(s_xagain[t % 2], 16 * (t // 2 + 1))
                if t == 0:
                    dve.wait_ge(s_wlo, 2)
                nc.vector.tensor_tensor(x2[:, t, :], banks[2 + t % 2][0:TT, :], x_again[:, t % 2, :],
                                        ALU.add).then_inc(s_x2, 1)

            def row_stats(src_rows, stage):
                for t in range(NT):
                    last = nc.vector.bn_stats(rst6[:, t, :], src_rows(t)).then_inc(s_rst, 1)
                for t in range(NT):
                    dve.wait_ge(s_rst, stage * NT + t + 1)
                    last = nc.vector.bn_aggr(rmv[:, t, :], rst6[:, t, :])
                link(last)
                nc.vector.tensor_scalar(rmv[:, :, 1], rmv[:, :, 1], EPS, None, ALU.add).then_inc(s_rmv, 1)
                dve.wait_ge(s_rr, stage + 1)

            dve.wait_ge(s_x2, NT)
            row_stats(lambda t: x2[:, t, :], 0)
            for t in range(NT):
                nc.vector.tensor_scalar(rows[:, t, 0:D], x2[:, t, :], rmv[:, t, 0:1], rrstd[:, t:t + 1],
                                        ALU.subtract, ALU.mult).then_inc(s_xf, 1)
            dve.wait_ge(s_xf, NT)
            row_stats(lambda t: rows[:, t, 0:D], 1)
            nc.vector.tensor_copy(rows[:, :, D], rmv[:, :, 0]).then_inc(s_rn, 1)
            dve.wait_ge(s_gate, 32)
            for t in range(NT):
                for e in range(NE):
                    i = t * NE + e
                    if i >= 2:
                        dve.wait_ge(s_logit, i - 1)
                    nc.vector.tensor_tensor_reduce(out=prod[:, i % 2, :], in0=rows[:, t, 0:D],
                                                   in1=gate[:, e * D:(e + 1) * D], scale=1.0,
                                                   scalar=gate_bias[:, e:e + 1], op0=ALU.mult, op1=ALU.add,
                                                   accum_out=logit[:, e, t:t + 1]).then_inc(s_logit, 1)
            dve.wait_ge(s_logit, NE * NT)
            for e in range(NE):
                mine = logit[:, e, :].unsqueeze(1)
                link(nc.vector.memset(beats[:, e, :, e:e + 1], 0.0))
                if e > 0:
                    nc.vector.tensor_tensor(beats[:, e, :, 0:e].rearrange("p t j -> p j t"), logit[:, 0:e, :],
                                            mine.broadcast_to([TT, e, NT]), ALU.is_ge)
                if e < NE - 1:
                    last = nc.vector.tensor_tensor(beats[:, e, :, e + 1:NE].rearrange("p t j -> p j t"),
                                                   logit[:, e + 1:NE, :],
                                                   mine.broadcast_to([TT, NE - 1 - e, NT]), ALU.is_gt)
            link(nc.vector.memset(tile_base[:, :, :, 0:1], 0.0))
            link(nc.vector.tensor_reduce(rank[:, :, :], beats[:, :, :, :], AX.X, ALU.add))
            for k in range(2):
                last = nc.vector.tensor_scalar(member[:, k, :, :], rank[:, :, :], float(k), None, ALU.is_equal)
            link(last)
            nc.vector.tensor_copy(member_h[:, :, :, :], member[:, :, :, :]).then_inc(s_member, 1)
            for k in range(2):
                last = nc.vector.tensor_tensor(masked[:, k, :, :], member[:, k, :, :], logit[:, :, :], ALU.mult)
            link(last)
            for k in range(2):
                last = nc.vector.tensor_reduce(best[:, k, :], masked[:, k, :, :].rearrange("p e t -> p t e"),
                                               AX.X, ALU.add)
            link(last)
            nc.vector.tensor_tensor(gap[:, 0, :], best[:, 1, :], best[:, 0, :], ALU.subtract).then_inc(s_gap, 1)
            dve.wait_ge(s_ex, 1)
            link(nc.vector.tensor_scalar(gap[:, 2, :], gap[:, 1, :], 1.0, None, ALU.add))
            link(nc.vector.reciprocal(gap[:, 3, :], gap[:, 2, :]))
            nc.vector.tensor_copy(probs[:, :, 0], gap[:, 3, :])
            nc.vector.tensor_tensor(probs[:, :, 1], gap[:, 1, :], gap[:, 3, :], ALU.mult)
            dve.wait_ge(s_pref, 1)
            dve.wait_ge(s_tot, 1)
            nc.vector.tensor_copy(before[:, :, :, :].rearrange("p k e t -> p (k e t)"),
                                  banks[0][0:TT, 0:2 * NE * NT])
            link(nc.vector.tensor_copy(tile_sum[:, :, :, :].rearrange("p k e t -> p (k e t)"),
                                       banks[1][:, 0:2 * NE * NT]))
            for t in range(NT):
                link(nc.vector.tensor_tensor(tile_base[:, :, :, t + 1], tile_base[:, :, :, t], tile_sum[:, :, :, t],
                                             ALU.add))
            link(nc.vector.tensor_tensor(before[:, :, :, :], before[:, :, :, :], tile_base[0:TT, :, :, 0:NT], ALU.add))
            link(nc.vector.tensor_tensor(before[:, 1, :, :], before[:, 1, :, :],
                                         tile_base[0:TT, 0, :, NT:NT + 1].broadcast_to([TT, NE, NT]), ALU.add))
            dve.wait_ge(s_tri, 5)
            for k in range(2):
                last = nc.vector.tensor_tensor(before[:, k, :, :], before[:, k, :, :], list0[:, :, :], ALU.add)
            link(last)
            link(nc.vector.tensor_tensor(masked[:, :, :, :], before[:, :, :, :], member[:, :, :, :], ALU.mult))
            for k in range(2):
                last = nc.vector.tensor_reduce(slot_f[:, k, :], masked[:, k, :, :].rearrange("p e t -> p t e"),
                                               AX.X, ALU.add)
            link(last)
            nc.vector.tensor_copy(slots[:, :, :].rearrange("p t k -> p k t"), slot_f[:, :, :]).then_inc(s_slots, 1)
            link(nc.vector.tensor_tensor(total[:, :], tile_base[:, 0, :, NT], tile_base[:, 1, :, NT], ALU.add))
            link(nc.vector.tensor_tensor(pad_f[:, :, :], pad_iota[:, :, :],
                                         total[:, :].unsqueeze(2).broadcast_to([P, NE, 2]), ALU.add))
            nc.vector.tensor_copy(pad_row[:, :, :], pad_f[:, :, :]).then_inc(s_pads, 1)
            link(nc.vector.memset(blocks_f[:, 0, :], 1.0))
            for b in range(1, NB):
                link(nc.vector.tensor_scalar(blocks_f[:, 1, :], total[0:1, :], float(b * LB), None, ALU.is_gt))
                link(nc.vector.tensor_tensor(blocks_f[:, 0, :], blocks_f[:, 0, :], blocks_f[:, 1, :], ALU.add))
            nc.vector.tensor_copy(nblocks[:, :], blocks_f[:, 0, :]).then_inc(s_nblocks, 1)
            dve.wait_ge(s_rr, 2)
            nc.vector.tensor_tensor(own[:, 0, :], tile_base[0:NE, 0, :, NT], ident[0:NE, 0:NE], ALU.mult)
            link(nc.vector.tensor_tensor(own[:, 1, :], total[0:NE, :], ident[0:NE, 0:NE], ALU.mult))
            link(nc.vector.tensor_reduce(bound[:, :], own[:, :, :], AX.X, ALU.add))
            nc.vector.tensor_scalar(in_grp[:, 0, :], pos[:, :], bound[:, 0:1], None, ALU.is_lt)
            link(nc.vector.tensor_scalar(in_grp[:, 1, :], pos[:, :], bound[:, 1:2], None, ALU.is_lt))
            link(nc.vector.tensor_tensor(in_grp[:, 1, :], in_grp[:, 1, :], in_grp[:, 0, :], ALU.subtract))
            link(nc.vector.tensor_scalar(marks[:, 0, :, :], in_grp[:, :, :], BIG, None, ALU.mult))
            nc.vector.tensor_scalar(marks[:, 1, :, :], in_grp[:, :, :], BIG, -BIG, ALU.mult,
                                    ALU.add).then_inc(s_marks, 1)

            dve.wait_ge(s_nblocks, 1)
            dve.wait_ge(s_routed, 1)
            dve.wait_ge(s_epar, 16)
            dve.wait_ge(s_econst, 9)
            dve.sem_inc(s_split, 2)
            dve.sem_inc(s_mx, 2)
            dve.sem_inc(s_oT, 1)
            dve.sem_inc(s_fin, 1)
            filled = Tally(dve, "dve_ppfilled", 0)
            taken = Tally(dve, "dve_taken", 2)
            seconds = Tally(dve, "dve_seconds", 0)
            steps = Tally(dve, "dve_steps", 0)
            scored = Tally(dve, "dve_scored", 0)
            maxed = Tally(dve, "dve_maxed", 2)
            scored_t = Tally(dve, "dve_scored_t", 1)
            on = Tally(dve, "dve_on", 2)
            biased = Tally(dve, "dve_biased", 0)
            heads = Tally(dve, "dve_heads", 1)
            counts = [heads, filled, taken, seconds, steps, scored, maxed, scored_t, on, biased]

            def step(ins):
                ins.then_inc(s_ech, 1)
                steps.skip(1)
                dve.wait_ge(s_ech, steps.at(0))

            def split_columns(t, count_at):
                dve.wait_ge(s_taken, taken.at(count_at))
                cols = slice(t * P, (t + 1) * P)
                src_t = t32[:, t % 2, :].rearrange("p (c n) -> p c n", c=KC)
                step(nc.vector.tensor_copy(hT[0][:, :, cols], src_t))
                nc.vector.tensor_tensor(hT[1][:, :, cols], src_t, hT[0][:, :, cols],
                                        ALU.subtract).then_inc(s_split, 1)

            def expert_dve(e, nb):
                spans, nt = spans_of(nb), 2 * nb
                ns = len(spans)
                nx = ns * nt
                for t in range(nt + 2):
                    if t < nt:
                        if t % 2 == 0:
                            dve.wait_ge(s_nr[t // 2], loaded[t // 2].at(16))
                            loaded[t // 2].skip(16)
                        nc.vector.tensor_scalar(v_rows[:, t, :], v_rows[:, t, :], v_stat[:, t, D:D + 1],
                                                v_stat[:, t, D + 1:D + 2], ALU.subtract, ALU.mult).then_inc(s_n1, 1)
                    if t >= 2:
                        split_columns(t - 2, t - 1)
                splits.skip(nt)
                taken.skip(2 * nt)
                filled.skip(2 * nt)
                for r in counts:
                    r.settle()

                def parameters(cols, j):
                    if isinstance(j, int):
                        mine = ep[:, BQ:L2W].rearrange("p (a j) -> p a j", a=3)[:, cols, j:j + 1]
                    else:
                        mine = ep[:, BQ:L2W].rearrange("p (a j) -> p a j", a=3)[:, cols, bass.ds(j, 1)]
                    return nc.vector.tensor_copy(ep_pair[:, cols].unsqueeze(2), mine)

                def split_pair():
                    for k in range(2 * ns):
                        s, side = k // 2, k % 2
                        c0, cn = spans[s]
                        cols = slice(c0, c0 + cn)
                        dve.wait_ge(s_taken, taken.at(k + 1))
                        high, low = halves[:, side, 0, cols], halves[:, side, 1, cols]
                        step(nc.vector.tensor_copy(high, t32[:, k % 2, 0:cn]))
                        nc.vector.tensor_tensor(low, t32[:, k % 2, 0:cn], high, ALU.subtract).then_inc(s_split, 1)
                        own, both = ((q_hi, q_both), (k_hi, k_both))[side]
                        nc.vector.tensor_copy(own[0:HD, 0, cols], high[0:HD])
                        nc.vector.tensor_copy(both[side * HD:(side + 1) * HD, 0, cols], high[0:HD])
                        dve.wait_ge(s_split, splits.at(k + 1))
                        last = nc.vector.tensor_copy(both[(1 - side) * HD:(2 - side) * HD, 0, cols], low[0:HD])
                        last.then_inc(s_qkd, 1)
                    taken.skip(3 * ns)
                    splits.skip(2 * ns)

                def second_head_copies():
                    before, parts = scored_t.at(0), splits.at(0)
                    dve.wait_ge(s_sT, before)
                    dve.wait_ge(s_split, parts)
                    cols = slice(0, nb * LB)
                    high, low = ([halves[HD:P, side, part, cols] for side in range(2)] for part in range(2))
                    nc.vector.tensor_copy(q_hi[0:HD, 1, cols], high[0])
                    nc.vector.tensor_copy(k_hi[0:HD, 1, cols], high[1])
                    nc.vector.tensor_copy(q_both[0:HD, 1, cols], high[0])
                    nc.vector.tensor_copy(k_both[0:HD, 1, cols], low[1])
                    nc.vector.tensor_copy(q_both[HD:P, 1, cols], low[0])
                    nc.vector.tensor_copy(k_both[HD:P, 1, cols], high[1]).then_inc(s_qkb, 1)

                def maximum(hd, i):
                    t, s = i // ns, i % ns
                    dve.wait_ge(s_s, scored.at(i + 1))
                    nc.vector.tensor_reduce(mx[:, hd, t, s:s + 1], sbk[i % 2][:, 0:spans[s][1]], AX.X,
                                            ALU.max).then_inc(s_mx, 1)
                    if i == nx - 1:
                        scored.skip(nx)
                        maxed.skip(nx)
                        dve.wait_ge(s_mx, maxed.at(0))
                        nc.vector.tensor_reduce(neg_max[:, hd, 0:nt], mx[:, hd, 0:nt, 0:ns], AX.X, ALU.max,
                                                negate=True).then_inc(s_neg, 1)

                def divide(j, s):
                    c0, cn = spans[s]
                    cols = slice(c0, c0 + cn)
                    pair = slice(j, j + 1) if isinstance(j, int) else bass.ds(j, 1)
                    o_hi, o_lo = (m[:, pair, cols] for m in oT)
                    mine = o_pair[:, cols].unsqueeze(1)
                    dve.wait_ge(s_on, on.at(ns + s + 1))
                    step(nc.vector.reciprocal(den[:, cols], den[:, cols]))
                    step(nc.vector.tensor_tensor(o_pair[:, cols], o_pair[:, cols], den[:, cols], ALU.mult))
                    step(nc.vector.tensor_scalar(o_hi, mine, ep_pair[:, 2:3], None, ALU.add))
                    nc.vector.scalar_tensor_tensor(o_lo, mine, ep_pair[:, 2:3], o_hi, ALU.add,
                                                   ALU.subtract).then_inc(s_oT, 1)

                def attend(j, hd, beside):
                    for i in range(nx):
                        if beside is not None:
                            for k in scores_beside(nx, i):
                                maximum(beside, k)
                        if hd == 1 and i % nt == 3 and i > nt:
                            divide(j, i // nt - 1)

                def finish(j):
                    divide(j, ns - 1)
                    on.skip(2 * ns)
                    heads.skip(ns)

                parameters(slice(0, 3), 0).then_inc(s_pair, 1)
                split_pair()
                for i in range(nx):
                    maximum(0, i)
                second_head_copies()
                for r in counts:
                    r.settle()
                with nc.vector.Fori(0, H // 2 - 1) as j:
                    parameters(slice(0, 2), j + 1).then_inc(s_pair, 1)
                    attend(j, 0, 1)
                    scored_t.skip(nx)
                    dve.wait_ge(s_sT, scored_t.at(0))
                    dve.wait_ge(s_qkb, seconds.at(1))
                    seconds.skip(1)
                    split_pair()
                    taken.skip(ns)
                    attend(j, 1, 0)
                    scored_t.skip(nx)
                    second_head_copies()
                    finish(j)
                    dve.wait_ge(s_oT, heads.at(0))
                    dve.sem_inc(s_idle, 1)
                    step(parameters(slice(2, 3), j + 1))
                    for r in counts:
                        r.settle()
                attend(H // 2 - 1, 0, 1)
                attend(H // 2 - 1, 1, None)
                finish(H // 2 - 1)
                scored_t.skip(2 * nx)
                taken.skip(ns)
                filled.skip(2 * H * ns)
                seconds.skip(1)
                dve.wait_ge(s_oT, heads.at(0))
                for t in range(nt):
                    dve.wait_ge(s_xb, biased.at(t + 1))
                    dve.wait_ge(s_pp, filled.at(t + 1))
                    nc.vector.tensor_tensor(v_rows[:, t, :], pp[t % 2][:, :], v_rows[:, t, :],
                                            ALU.add).then_inc(s_taken, 1)
                    if t > 0:
                        dve.wait_ge(s_taken, taken.at(t))
                        nc.vector.bn_stats(l2st[:, t - 1, :], v_rows[:, t - 1, :])
                dve.wait_ge(s_taken, taken.at(nt))
                step(nc.vector.bn_stats(l2st[:, nt - 1, :], v_rows[:, nt - 1, :]))
                dve.sem_inc(s_idle, 1)
                biased.skip(nt)
                taken.skip(nt)
                filled.skip(nt)
                for t in range(nt):
                    last = nc.vector.bn_aggr(l2mv[:, t, :], l2st[:, t, :])
                step(last)
                nc.vector.tensor_scalar(l2mv[:, 0:nt, 1], l2mv[:, 0:nt, 1], EPS, None, ALU.add).then_inc(s_l2v, 1)
                dve.wait_ge(s_l2r, e + 1)
                for t in range(nt):
                    if t >= 2:
                        dve.wait_ge(s_pp, filled.at(t - 1))
                    nc.vector.tensor_scalar(n2[:, t % 2, :], v_rows[:, t, :], l2mv[:, t, 0:1], l2r[:, t:t + 1],
                                            ALU.subtract, ALU.mult).then_inc(s_n2, 1)
                    if t >= 1:
                        split_columns(t - 1, t)
                split_columns(nt - 1, nt)
                taken.skip(nt)
                filled.skip(nt)
                for k in range(2 * ns):
                    hc, (c0, cn) = k // ns, spans[k % ns]
                    dve.wait_ge(s_taken, taken.at(k + 1))
                    step(nc.vector.tensor_copy(hid[0][:, hc, c0:c0 + cn], t32[:, k % 2, 0:cn]))
                    nc.vector.tensor_tensor(hid[1][:, hc, c0:c0 + cn], t32[:, k % 2, 0:cn],
                                            hid[0][:, hc, c0:c0 + cn], ALU.subtract).then_inc(s_split, 1)
                taken.skip(2 * ns)
                filled.skip(2 * ns)
                for t in range(nt):
                    dve.wait_ge(s_xb, biased.at(t + 1))
                    dve.wait_ge(s_pp, filled.at(t + 1))
                    last = nc.vector.tensor_tensor(v_rows[:, t, :], pp[t % 2][:, :], v_rows[:, t, :],
                                                   ALU.add).then_inc(s_taken, 1)
                biased.skip(nt)
                taken.skip(nt)
                filled.skip(nt)
                dve.wait_ge(s_taken, taken.at(0))
                dve.sem_inc(s_fin, 1)
                splits.skip(nt + 2 * ns)
                for r in counts:
                    r.settle()

            splits = Tally(dve, "dve_splits", 2)
            loaded = [Tally(dve, f"dve_loaded{b}", 0) for b in range(NB)]
            counts += [splits] + loaded
            with nc.vector.Fori(0, NE) as e:
                nb_e = nc.vector.value_load(nblocks[0:1, bass.ds(e, 1)], min_val=1, max_val=NB)
                step(nc.vector.tensor_copy(ep[:, :].unsqueeze(1), epar[:, bass.ds(e, 1), :]))
                nc.vector.tensor_scalar(ep[:, BQ:BK], ep[:, BQ:BK], HD ** -0.5, None, ALU.mult).then_inc(s_ep, 1)
                steps.settle()
                for nb in range(1, NB + 1):
                    with nc.vector.If(nb_e == nb):
                        expert_dve(e, nb)

            for t in range(NT):
                dve.wait_ge(s_xy[t % 2], 16 * (t // 2 + 1))
                dve.wait_ge(s_g[t % 2], 32 * (t // 2 + 1))
                if t >= 2:
                    dve.wait_ge(s_yout[t % 2], 16 * (t // 2))
                y = n2[0:TT, t % 2, :]
                step(nc.vector.scalar_tensor_tensor(y, probs_t[0:TT, 2 * (t % 2), :], probs[:, t, 0:1],
                                                    t32[0:TT, t % 2, :], ALU.mult, ALU.add))
                nc.vector.scalar_tensor_tensor(y, probs_t[0:TT, 2 * (t % 2) + 1, :], probs[:, t, 1:2], y,
                                               ALU.mult, ALU.add).then_inc(s_y, 1)


_INS = ['x', 'src', 'dst', 'gnn_w', 'gnn_par', 'gate_w', 'gate_b', 'ew', 'epar', 'erow']
_OUTS = [((N, D), 'float32')]


def kernel(**inputs):
    import numpy as _np
    import concourse.bacc as _bacc
    from concourse import mybir as _mybir
    from concourse.bass_utils import run_bass_kernel_spmd as _run

    def chunked(v):
        return v.reshape(-1, P).T

    def by_chunk(w):
        w = w.transpose(0, 2, 1)
        return w.reshape(NE, -1, P, w.shape[2]).transpose(0, 2, 1, 3).reshape(NE, P, -1)

    a = {k: _np.asarray(v) for k, v in inputs.items()}
    lay = {
        'x': a['x'],
        'src': a['src'].reshape(NCH, TT).T,
        'dst': a['dst'].reshape(NCH, TT).T,
        'gnn_w': _np.concatenate([a[k].T.reshape(KC, P, D).transpose(1, 0, 2).reshape(P, KC * D)
                                  for k in ('L0_gnn_W_l', 'L0_gnn_W_r')], 1),
        'gnn_par': _np.stack([chunked(a[k]) for k in ('L0_gnn_b_l', 'L0_gnn_gamma', 'L0_gnn_beta')], 1),
        'gate_w': a['L0_ffn_gate_w'],
        'gate_b': a['L0_ffn_gate_b'].reshape(1, NE),
        'ew': _np.concatenate([by_chunk(a['L0_ffn_' + k]) for k in ('in_proj_w', 'out_proj_w', 'mlp_w1', 'mlp_w2')], 2),
        'epar': _np.concatenate([a['L0_ffn_' + k].reshape(NE, -1, P).transpose(2, 0, 1) for k in (
            'ln1_w', 'ln1_b', 'in_proj_b', 'ln2_w', 'ln2_b', 'mlp_b1')], 2),
        'erow': _np.stack([a['L0_ffn_out_proj_b'], a['L0_ffn_mlp_b2']], 1),
    }
    nc = _bacc.Bacc("TRN2", target_bir_lowering=False, num_devices=1)
    arrays, args = {}, []
    for name in _INS:
        v = _np.ascontiguousarray(lay[name])
        arrays[f"in_{name}_dram"] = v
        args.append(nc.dram_tensor(f"in_{name}_dram", v.shape, _mybir.dt.from_np(v.dtype), kind="ExternalInput").ap())
    for i, (shape, dtype) in enumerate(_OUTS):
        dt = _mybir.dt.from_np(_np.dtype(dtype))
        args.append(nc.dram_tensor(f"out_{i}_dram", shape, dt, kind="ExternalOutput").ap())
    program(nc, *args)
    r = _run(nc, [arrays], core_ids=[0])
    return r.results[0]["out_0_dram"]
```
